# Optimizing a Trainium2 kernel written in Bass

```python
import numpy as np
import jax
import jax.numpy as jnp

def _softmax(x, axis=-1):
    return jax.nn.softmax(x, axis=axis)

def _gelu(x):
    return jax.nn.gelu(x, approximate=True)

def _silu(x):
    return jax.nn.silu(x)

def _sigmoid(x):
    return jax.nn.sigmoid(x)

def _layernorm(x, axis=-1, eps=1e-05):
    m = jnp.mean(x, axis=axis, keepdims=True)
    v = jnp.var(x, axis=axis, keepdims=True)
    return (x - m) / jnp.sqrt(v + eps)

def _scatter_add(tgt, idx, src, axis=0):
    return tgt.at[idx].add(src)

def _segment_sum(src, seg, n):
    return jax.ops.segment_sum(src, seg, n)
kernel_name = 'mk_gnn_ffn_d1_gnn_r8_1d9767'

def setup_inputs(seed: int=0):
    np.random.seed(seed)
    _w = jnp.asarray

    def _rec_inputs():
        import jax
        import jax.numpy as jnp
        _gk = jax.random.key(seed)
        x = -0.000364 + 1 * jax.random.normal(jax.random.fold_in(_gk, 1), (1250, 768), jnp.float32)
        src = jax.random.randint(jax.random.fold_in(_gk, 2), (40000,), 0, 1250, jnp.int32)
        dst = jax.random.randint(jax.random.fold_in(_gk, 3), (40000,), 0, 1250, jnp.int32)
        _o = jnp.argsort(dst, stable=True)
        src = src[_o]
        dst = dst[_o]
        return (x, src, dst)
    x, src, dst = _rec_inputs()

    def _L0_gnn_setup():
        import jax, jax.numpy as jnp
        import numpy as np
        N = 2500
        E_RAND = 40000
        NEG_SLOPE = 0.2

        def gat_layer(x, W, a_src, a_dst, bias, src, dst, heads, out_c, concat):
            n = x.shape[0]
            h = (x @ W).reshape(n, heads, out_c)
            al_s = jnp.einsum('nhc,hc->nh', h, a_src)
            al_d = jnp.einsum('nhc,hc->nh', h, a_dst)
            e = jax.nn.leaky_relu(al_s[src] + al_d[dst], NEG_SLOPE)
            m = jax.ops.segment_max(e, dst, num_segments=n)
            ex = jnp.exp(e - m[dst])
            z = jax.ops.segment_sum(ex, dst, num_segments=n)
            alpha = ex / (z[dst] + 1e-16)
            msg = h[src] * alpha[:, :, None]
            out = jax.ops.segment_sum(msg, dst, num_segments=n)
            out = out.reshape(n, heads * out_c) if concat else out.mean(axis=1)
            return out + bias
        key = jax.random.key(seed)
        ks = jax.random.split(key, 10)
        x = jax.random.normal(ks[0], (N, 768), dtype=jnp.float32)
        src = jax.random.randint(ks[1], (E_RAND,), 0, N)
        dst = jax.random.randint(ks[2], (E_RAND,), 0, N)
        loop = jnp.arange(N)
        edge_index = jnp.stack([jnp.concatenate([src, loop]), jnp.concatenate([dst, loop])])
        s = 1.0 / np.sqrt(768.0)
        W1 = jax.random.normal(ks[3], (768, 768), dtype=jnp.float32) * s
        a_src1 = jax.random.normal(ks[4], (8, 96), dtype=jnp.float32) * 0.1
        a_dst1 = jax.random.normal(ks[5], (8, 96), dtype=jnp.float32) * 0.1
        b1 = jnp.zeros((768,), dtype=jnp.float32)
        W2 = jax.random.normal(ks[6], (768, 768), dtype=jnp.float32) * s
        a_src2 = jax.random.normal(ks[7], (1, 768), dtype=jnp.float32) * 0.1
        a_dst2 = jax.random.normal(ks[8], (1, 768), dtype=jnp.float32) * 0.1
        b2 = jnp.zeros((768,), dtype=jnp.float32)
        return {'x': x, 'edge_index': edge_index, 'W1': W1, 'a_src1': a_src1, 'a_dst1': a_dst1, 'b1': b1, 'W2': W2, 'a_src2': a_src2, 'a_dst2': a_dst2, 'b2': b2}
    _L0_gnn_all = _L0_gnn_setup()
    _L0_gnn_in = {k: v for k, v in _L0_gnn_all.items() if k in ('W1', 'a_src1', 'a_dst1', 'b1', 'W2', 'a_src2', 'a_dst2', 'b2')}
    del _L0_gnn_all

    def _L0_ffn_setup():
        import jax, jax.numpy as jnp
        import numpy as np
        EPS_NORM = 1e-06
        EPS_LN = 1e-05

        def _layernorm(x, g, b):
            mu = jnp.mean(x, axis=-1, keepdims=True)
            var = jnp.mean(jnp.square(x - mu), axis=-1, keepdims=True)
            return (x - mu) * jax.lax.rsqrt(var + EPS_LN) * g + b
        key = jax.random.key(seed)
        ks = jax.random.split(key, 6)
        b, m, d = (8, 1024, 768)
        n, p = (64, 16)
        h = 2 * d
        x = jax.random.normal(ks[0], (b, m, d), dtype=jnp.float32)
        phi = jax.random.normal(ks[1], (n, p, d), dtype=jnp.float32)
        ln_g = jnp.ones((n, d), dtype=jnp.float32)
        ln_b = jnp.zeros((n, d), dtype=jnp.float32)
        w1 = jax.random.normal(ks[2], (n, d, h), dtype=jnp.float32) * (1.0 / np.sqrt(d))
        b1 = jax.random.normal(ks[3], (n, h), dtype=jnp.float32) * 0.01
        w2 = jax.random.normal(ks[4], (n, h, d), dtype=jnp.float32) * (1.0 / np.sqrt(h))
        b2 = jax.random.normal(ks[5], (n, d), dtype=jnp.float32) * 0.01
        return {'x': x, 'phi': phi, 'ln_g': ln_g, 'ln_b': ln_b, 'w1': w1, 'b1': b1, 'w2': w2, 'b2': b2}
    _L0_ffn_all = _L0_ffn_setup()
    _L0_ffn_in = {k: v for k, v in _L0_ffn_all.items() if k in ('phi', 'ln_g', 'ln_b', 'w1', 'b1', 'w2', 'b2')}
    del _L0_ffn_all
    return {'x': x, 'src': src, 'dst': dst, 'L0_gnn_W1': _L0_gnn_in['W1'], 'L0_gnn_a_src1': _L0_gnn_in['a_src1'], 'L0_gnn_a_dst1': _L0_gnn_in['a_dst1'], 'L0_gnn_b1': _L0_gnn_in['b1'], 'L0_gnn_W2': _L0_gnn_in['W2'], 'L0_gnn_a_src2': _L0_gnn_in['a_src2'], 'L0_gnn_a_dst2': _L0_gnn_in['a_dst2'], 'L0_gnn_b2': _L0_gnn_in['b2'], 'L0_ffn_phi': _L0_ffn_in['phi'], 'L0_ffn_ln_g': _L0_ffn_in['ln_g'], 'L0_ffn_ln_b': _L0_ffn_in['ln_b'], 'L0_ffn_w1': _L0_ffn_in['w1'], 'L0_ffn_b1': _L0_ffn_in['b1'], 'L0_ffn_w2': _L0_ffn_in['w2'], 'L0_ffn_b2': _L0_ffn_in['b2']}

def reference(x, src, dst, L0_gnn_W1, L0_gnn_a_src1, L0_gnn_a_dst1, L0_gnn_b1, L0_gnn_W2, L0_gnn_a_src2, L0_gnn_a_dst2, L0_gnn_b2, L0_ffn_phi, L0_ffn_ln_g, L0_ffn_ln_b, L0_ffn_w1, L0_ffn_b1, L0_ffn_w2, L0_ffn_b2):
    import jax
    import jax.numpy as jnp

    def _L0_gnn_ref(x, edge_index, W1, a_src1, a_dst1, b1, W2, a_src2, a_dst2, b2):
        import jax, jax.numpy as jnp
        import numpy as np
        N = 2500
        E_RAND = 40000
        NEG_SLOPE = 0.2

        def gat_layer(x, W, a_src, a_dst, bias, src, dst, heads, out_c, concat):
            n = x.shape[0]
            h = (x @ W).reshape(n, heads, out_c)
            al_s = jnp.einsum('nhc,hc->nh', h, a_src)
            al_d = jnp.einsum('nhc,hc->nh', h, a_dst)
            e = jax.nn.leaky_relu(al_s[src] + al_d[dst], NEG_SLOPE)
            m = jax.ops.segment_max(e, dst, num_segments=n)
            ex = jnp.exp(e - m[dst])
            z = jax.ops.segment_sum(ex, dst, num_segments=n)
            alpha = ex / (z[dst] + 1e-16)
            msg = h[src] * alpha[:, :, None]
            out = jax.ops.segment_sum(msg, dst, num_segments=n)
            out = out.reshape(n, heads * out_c) if concat else out.mean(axis=1)
            return out + bias
        src, dst = (edge_index[0], edge_index[1])
        h = gat_layer(x, W1, a_src1, a_dst1, b1, src, dst, heads=8, out_c=96, concat=True)
        h = jax.nn.elu(h)
        out = gat_layer(h, W2, a_src2, a_dst2, b2, src, dst, heads=1, out_c=768, concat=False)
        return out

    def _L0_ffn_ref(x, phi, ln_g, ln_b, w1, b1, w2, b2):
        import jax, jax.numpy as jnp
        import numpy as np
        EPS_NORM = 1e-06
        EPS_LN = 1e-05

        def _layernorm(x, g, b):
            mu = jnp.mean(x, axis=-1, keepdims=True)
            var = jnp.mean(jnp.square(x - mu), axis=-1, keepdims=True)
            return (x - mu) * jax.lax.rsqrt(var + EPS_LN) * g + b
        phi_n = phi * jax.lax.rsqrt(jnp.sum(jnp.square(phi), axis=0, keepdims=True) + EPS_NORM)
        bsz, m, d = x.shape
        n, p, _ = phi_n.shape
        logits = jnp.einsum('bmd,npd->bmnp', x, phi_n)
        D = jax.nn.softmax(logits, axis=1)
        C = jax.nn.softmax(logits.reshape(bsz, m, n * p), axis=-1)
        Xs = jnp.einsum('bmd,bmnp->bnpd', x, D)
        hdn = _layernorm(Xs, ln_g[:, None, :], ln_b[:, None, :])
        hdn = jnp.einsum('bnpd,ndh->bnph', hdn, w1) + b1[:, None, :]
        hdn = jax.nn.gelu(hdn, approximate=False)
        Ys = jnp.einsum('bnph,nhd->bnpd', hdn, w2) + b2[:, None, :]
        Ys = Ys.reshape(bsz, n * p, d)
        Y = jnp.einsum('bsd,bms->bmd', Ys, C)
        return Y
    edge_index = jnp.stack([src, dst])
    x = x + _L0_gnn_ref(_layernorm(x, axis=-1), edge_index, L0_gnn_W1, L0_gnn_a_src1, L0_gnn_a_dst1, L0_gnn_b1, L0_gnn_W2, L0_gnn_a_src2, L0_gnn_a_dst2, L0_gnn_b2)
    x = x + _L0_ffn_ref(_layernorm(x, axis=-1)[None], L0_ffn_phi, L0_ffn_ln_g, L0_ffn_ln_b, L0_ffn_w1, L0_ffn_b1, L0_ffn_w2, L0_ffn_b2)[0]
    return x

_drawn_inputs = setup_inputs


def setup_inputs(seed=0):
    import zlib

    import numpy as np

    out = dict(_drawn_inputs(seed))
    spreads = {'L0_gnn_b1': (0.0, 0.1),
     'L0_gnn_b2': (0.0, 0.1),
     'L0_ffn_ln_g': (1.0, 0.2),
     'L0_ffn_ln_b': (0.0, 0.1)}
    factors = {'L0_gnn_a_dst1': 4.86, 'L0_gnn_a_dst2': 7.323, 'L0_ffn_b1': 8.0, 'L0_ffn_b2': 7.31}
    for name, (base, spread) in spreads.items():
        noise = np.random.default_rng([zlib.crc32(name.encode()), seed]).standard_normal(out[name].shape)
        drawn = base * np.exp(spread * noise) if base else spread * noise
        out[name] = jnp.asarray(drawn.astype(out[name].dtype))
    for name, factor in factors.items():
        out[name] = (out[name] * factor).astype(out[name].dtype)
    return out
```

```python
from contextlib import ExitStack

import concourse.bass as bass
from concourse import mybir
from concourse.alu_op_type import AluOpType as ALU

F32 = mybir.dt.float32
BF16 = mybir.dt.bfloat16
F16 = mybir.dt.float16
U16 = mybir.dt.uint16
I32 = mybir.dt.int32
ACT = mybir.ActivationFunctionType
AX_X = mybir.AxisListType.X
RMAX = bass.bass_isa.ReduceOp.max

NODES = 1250
NP = 125
NT = NODES // NP
D = 768
KD = D // 128
HALF = D // 2
HEADS = 8
HC = D // HEADS
EDGES = 40000
NGROUP = 40
ECH = EDGES // NGROUP // NP
WIN = 50
NWIN = NODES // WIN
SLOPE = 0.2
NO_EDGE = -1e30
MAX_FLOOR = -1e20
EPS_LN = 1e-5
EPS_PHI = 1e-6
EPS_Z = 1e-16
NEXP = 64
PSLOT = 16
SLOTS = NEXP * PSLOT
ST = SLOTS // 128
GE = NEXP // ST
HID = 2 * D
KH = HID // 128
QUAD = 4
SUB = GE // QUAD
RING = 3
RW = QUAD * HID
USES = KD * SUB
PADDED = 3 * PSLOT
NPB = 3


class Chain:

    def __init__(self, eng, sem):
        self.eng, self.sem, self.n, self.base, self.turn = eng, sem, 0, 0, 0

    def step(self, ins):
        ins.then_inc(self.sem, 1)
        self.n += 1
        self.eng.wait_ge(self.sem, self.turn + self.base + self.n)

    def enter(self, i, per):
        self.start, self.per, self.turn = self.n, per, i * per

    def leave(self, count):
        assert self.n - self.start == self.per, (self.n - self.start, self.per)
        self.n, self.turn = self.start, 0
        if isinstance(count, int):
            self.n += count * self.per
        else:
            self.base = count * self.per


def gnn_ffn(nc, x, src, dst, W1, a_src1, a_dst1, b1, W2, a_src2, a_dst2, b2,
            phi, ln_g, ln_b, w1, fb1, w2, fb2, out):
    with ExitStack() as ctx:
        WORDS = 53200
        arena = ctx.enter_context(nc.sbuf_tensor("arena", [128, WORDS], F32))
        ps = ctx.enter_context(nc.psum_tensor("ps", [128, 8, 512], F32))

        def sem(name):
            return ctx.enter_context(nc.semaphore(name))

        def at(off, *shape, parts=128, dtype=F32):
            n = 1
            for s in shape:
                n *= s
            size = 2 if dtype in (BF16, F16, U16) else 4
            words = (n * size + 3) // 4
            assert off + words <= WORDS, (off, words)
            v = arena[0:parts, off:off + words]
            if dtype != F32:
                v = v.bitcast(dtype)
            v = v[:, 0:n]
            if len(shape) == 2:
                v = v.rearrange("p (a b) -> p a b", b=shape[1])
            elif len(shape) == 3:
                v = v.rearrange("p (a b c) -> p a b c", b=shape[1], c=shape[2])
            elif len(shape) == 4:
                v = v.rearrange("p (a b c d) -> p a b c d", b=shape[1], c=shape[2], d=shape[3])
            return v

        H1 = at(0, NT, HEADS, HC + 1, parts=NP)
        CNT_OFF = 7760
        CNT3 = at(CNT_OFF, NT, NODES + WIN, parts=NP, dtype=U16)
        ALS_OFF = CNT_OFF + 6500
        ALS = at(ALS_OFF, HEADS, NODES, parts=NP)
        ALS2 = at(ALS_OFF + 6200, NODES, parts=NP)
        E_OFF = ALS_OFF + 10000
        X = at(E_OFF, NT, D, parts=NP)
        H2 = at(E_OFF, NT, D + 1, parts=NP)
        F_OFF = E_OFF + 7690
        NEGC = at(F_OFF, NODES, parts=NP, dtype=BF16)
        NEGS = at(F_OFF + 625, NT, NODES, parts=NP, dtype=BF16)
        neg_dram = nc.dram_tensor("neg_dram", (NT, NP, NODES), BF16, kind="Internal").ap()
        G_OFF = F_OFF + 6875
        W1A = at(G_OFF, KD, 2, HALF + 8)
        W2A = at(G_OFF, KD, 2, HALF + 1)
        WK = G_OFF + 4704
        TR = [at(WK + 1250 * r, NODES, parts=NP) for r in range(4)]
        TS = [at(F_OFF + 1875 + 1250 * r, NODES, parts=NP) for r in range(2)]
        PR = [at(WK + 5000, NT, NP, parts=NP), at(F_OFF + 4375, NT, NP, parts=NP)]
        O1 = at(WK + 6250, D, parts=NP)
        O1T = at(WK + 7018, KD, NP)
        B1R = at(WK + 7768, D, parts=NP)
        SM = WK + 8536
        IDENT = at(SM, 128)
        ALD = at(SM + 128, NT, HEADS, parts=NP)
        ALD2 = at(SM + 208, NT, parts=NP)
        M0 = at(SM + 218, HEADS, parts=NP)
        TN = at(SM + 226, HEADS, parts=NP)
        NM = at(SM + 234, HEADS, parts=NP)
        NL = at(SM + 320, HEADS, parts=NP)
        ALU8 = at(SM + 328, NT, HEADS, parts=NP)
        ALU8B = at(SM + 408, NT, parts=NP)
        RZ = at(SM + 242, HEADS, parts=NP)
        ALSN = [at(SM + 250 + 8 * s, HEADS, parts=NP) for s in range(2)]
        MV = at(SM + 266, NT, 2, parts=NP)
        MV1 = at(SM + 418, 2, parts=NP)
        BS2 = at(SM + 420, 2, 6, parts=NP)
        ALS2N = at(SM + 306, NT, parts=NP)
        STD = at(SM + 286, NT, parts=NP)
        RSTD = at(SM + 296, NT, parts=NP)
        XH = [at(WK + 768 * s, D, parts=NP) for s in range(2)]
        XT = [at(WK + 1536 + 750 * s, KD, NP) for s in range(2)]
        AVEC = [at(WK + 3036 + 768 * s, 2, HALF) for s in range(2)]
        BST = at(WK + 4600, NT, 2, 6, parts=NP)
        SRCI = at(F_OFF, NGROUP, ECH, parts=NP, dtype=I32)
        DSTI = at(F_OFF + 320, NGROUP, ECH, parts=NP, dtype=I32)
        SRCF = at(F_OFF + 640, NGROUP * ECH, parts=NP)
        DSTF = at(F_OFF + 960, NGROUP, ECH, parts=NP)
        TA = at(F_OFF + 1280, NGROUP * ECH, parts=NP)
        KEYB = at(F_OFF + 1600, NGROUP * ECH, parts=NP)
        KEYA = at(F_OFF + 1920, NGROUP, ECH, parts=NP)
        KEY = at(F_OFF + 2240, NGROUP, ECH, parts=NP)
        TD = at(F_OFF + 2560, NGROUP, ECH, parts=NP)
        MK = at(F_OFF + 2880, NGROUP, ECH, parts=NP)
        GST = at(F_OFF + 3200, 2, NGROUP, parts=NP)
        GAR = at(F_OFF + 3280, 2, NGROUP, parts=NP)
        SPAN = at(F_OFF + 3360, NGROUP, parts=NP)
        FLG = at(F_OFF + 3400, 2, parts=NP)
        D0 = at(F_OFF + 3404, NGROUP, parts=NP)
        D0I = at(F_OFF + 3444, NGROUP, parts=NP, dtype=I32)
        WPI = at(F_OFF + 3484, 1, parts=NP, dtype=I32)
        IOI = at(F_OFF + 3500, NT * WIN, parts=NP, dtype=I32)
        IOB = at(F_OFF + 4000, 128, parts=NP, dtype=F16)
        IOK = at(F_OFF + 4064, NT * WIN, parts=NP, dtype=F16)
        OHR = 4
        OB = [at(F_OFF + 4320 + 64 * r, 128, parts=NP, dtype=F16) for r in range(OHR)]
        OK = [at(F_OFF + 4576 + 250 * r, NT * WIN, parts=NP, dtype=F16) for r in range(OHR)]
        CF = [at(WK + 1250 * r, NT, NP, parts=NP) for r in range(2)]
        AW = [at(768 * r, 2, HALF) for r in range(2)]
        AW2 = [at(WK + 6250, 2, HALF), at(WK + 5000, 2, HALF)]
        EL = at(WK + 5000, D, parts=NP)
        PHR = at(ALS_OFF, ST, D)
        B2R = at(WK + 7768, D, parts=NP)

        X2 = at(0, NT, D, parts=NP)
        CT_OFF = 7760
        CT = at(CT_OFF, ST, NODES)
        XH2_OFF = CT_OFF + 10000
        XH2 = at(XH2_OFF, NT, D + 1, parts=NP)
        L_OFF = XH2_OFF + 7690
        L = at(L_OFF, NT, SLOTS, parts=NP)
        PHT_OFF = XH2_OFF + RING * RW
        assert PHT_OFF >= L_OFF + NT * SLOTS
        PHT = at(PHT_OFF, KD, SLOTS)
        XGT = at(PHT_OFF, KD, SLOTS)
        CM_OFF = PHT_OFF + 6144
        CMB = at(CM_OFF, SLOTS, parts=NP)
        PRE_OFF = CM_OFF + 1024
        GT = at(PRE_OFF, KD, NEXP)
        BT = at(PRE_OFF + 1152, KD, NEXP)
        FB1T = at(PRE_OFF + 384, KH, NEXP)
        FW = PRE_OFF + 1536
        XC = [at(FW + 768 * s, D, parts=NP) for s in range(2)]
        XCT = [at(FW + 1536 + 750 * s, KD, NP) for s in range(2)]
        XSW = at(FW, D)
        LC = [at(FW + 3040, SLOTS, parts=NP), at(FW + 5988, SLOTS, parts=NP)]
        CC = [at(FW + 4064, SLOTS, parts=NP), at(CM_OFF, SLOTS, parts=NP)]
        DIAG = at(FW + 3040, ST, 128)
        DC = [at(FW + 1536, NT, 128, parts=NP), at(FW + 2816, NT, 128, parts=NP)]
        SM2 = FW + 5088
        assert SM2 + 900 + SLOTS <= SM, (SM2, SM)
        CMX = at(SM2, ST, NT)
        CMN = at(SM2 + 80, ST)
        ONES = at(SM2 + 230, 128)
        NRM = at(SM2 + 360, KD, PSLOT)
        NRR = at(SM2 + 456, KD, PSLOT)
        RM = [at(SM2 + 580 + s, 1, parts=NP) for s in range(2)]
        RS = [at(SM2 + 582 + s, 1, parts=NP) for s in range(2)]
        RI = [at(SM2 + 584 + s, 1, parts=NP) for s in range(2)]
        CSI = at(SM2 + 555, 1)
        SST = at(SM2 + 556, 2, 6)
        SMV = at(SM2 + 568, 2)
        SSD = at(SM2 + 570, 1)
        SRD = at(SM2 + 571, 1)
        SQ = [at(FW, SLOTS), at(FW + 1024, SLOTS)]
        LDP = [at(FW + 2048, D, parts=NEXP), at(FW + 2816, D, parts=NEXP)]
        LDB = at(L_OFF, HID, parts=NEXP)
        RG = [at(XH2_OFF + RW * s, QUAD, HID) for s in range(RING)]
        CTC = at(CM_OFF, NODES)
        XGS = at(FW - 128, KD, QUAD, PADDED)
        HTS = at(FW + 1024, KH, QUAD, PADDED)
        HS = at(FW + 3328, HID)
        HB = at(FW + 4864, KH, 128)
        YS = at(SM + 128, D)
        B2G = at(FW + 6400, D)
        assert CM_OFF + NODES <= PRE_OFF + 384 and FW + 7168 <= SM

        L1_STEPS = 2 * HEADS + 7

        def PST(k, n, bank):
            v = ps[:, bank:min(bank + 3, 8), :].rearrange("p a (b n) -> p (a b) n", n=128)
            return v[:, k:k + n, 0:NP]

        def PSW(bank, n, width=128):
            return ps[:, bank:bank + 2, :].rearrange("p a (b n) -> p (a b) n", n=128)[:, 0:n, 0:width]

        def pairs(v, k):
            return v.rearrange("p (c n j) -> p c j n", j=2, n=128)[:, k // 2, k % 2, :]

        def w1_done(g):
            return RING + USES if isinstance(g, int) and g == 0 else g * (2 * USES) + RING

        def w2_done(g):
            return RING + 2 * ST * USES if isinstance(g, int) and g == ST - 1 else g * (2 * USES) + (RING + 3 * USES)

        x_in = sem("x_in"); w1_in = sem("w1_in"); avec_in = sem("avec_in"); edges_in = sem("edges_in")
        b1row_in = sem("b1row_in"); w2_in = sem("w2_in"); avec2_in = sem("avec2_in"); x_again = sem("x_again")
        b2row_in = sem("b2row_in"); phi_in = sem("phi_in"); par_in = sem("par_in"); fb1_in = sem("fb1_in")
        ident_ready = sem("ident_ready"); iota_ready = sem("iota_ready"); cnt_zero = sem("cnt_zero")
        dve_c = sem("dve_c"); count_c = sem("count_c"); attend_c = sem("attend_c"); act_c = sem("act_c"); pool_c = sem("pool_c")
        span_ready = sem("span_ready"); span_all = sem("span_all"); windows_ready = sem("windows_ready")
        wa_ready = sem("wa_ready"); h1_ones = sem("h1_ones")
        var_ready = sem("var_ready"); std_ready = sem("std_ready")
        xhat_ready = sem("xhat_ready"); xT_psum = sem("xT_psum"); xT_ready = sem("xT_ready")
        h1_psum = sem("h1_psum"); h1_stored = sem("h1_stored"); als_psum = sem("als_psum"); als_stored = sem("als_stored")
        onehot_ready = sem("onehot_ready"); chunk_counted = sem("chunk_counted"); group_added = sem("group_added"); cnt_done = sem("cnt_done"); keys_known = sem("keys_known"); slot_taken = sem("slot_taken")
        cnt_tile = sem("cnt_tile"); cntT_psum = sem("cntT_psum"); neg_ready = sem("neg_ready")
        neg_in = sem("neg_in"); neg_saved = sem("neg_saved"); upper_ready = sem("upper_ready"); summed = sem("summed"); ald_scaled = sem("ald_scaled"); masked = sem("masked"); shift_ready = sem("shift_ready")
        e_ready = sem("e_ready"); eT_psum = sem("eT_psum"); p_ready = sem("p_ready"); o_psum = sem("o_psum")
        rows_done = sem("rows_done")
        elu_in = sem("elu_in"); elu_exp = sem("elu_exp"); o1_ready = sem("o1_ready")
        o1T_psum = sem("o1T_psum"); o1T_ready = sem("o1T_ready"); h2_psum = sem("h2_psum"); h2_stored = sem("h2_stored")
        als2_psum = sem("als2_psum"); als2_stored = sem("als2_stored"); wa2_ready = sem("wa2_ready"); h2_ones = sem("h2_ones")
        neg2_in = sem("neg2_in"); upper2_ready = sem("upper2_ready"); summed2 = sem("summed2"); ald2_scaled = sem("ald2_scaled"); masked2 = sem("masked2"); shift2_ready = sem("shift2_ready")
        e2_ready = sem("e2_ready"); eT2_psum = sem("eT2_psum"); p2_ready = sem("p2_ready"); o2_psum = sem("o2_psum")
        x2_ready = sem("x2_ready"); xb_ready = sem("xb_ready")
        phT_psum = sem("phT_psum"); phT_stored = sem("phT_stored"); nrm_ready = sem("nrm_ready"); ones_ready = sem("ones_ready")
        second_c = sem("second_c"); expert_c = sem("expert_c"); logit_c = sem("logit_c"); input_c = sem("input_c"); nrs_ready = sem("nrs_ready")
        phn_ready = sem("phn_ready"); par_psum = sem("par_psum"); par_stored = sem("par_stored")
        var2_ready = sem("var2_ready"); std2_ready = sem("std2_ready")
        xc_ready = sem("xc_ready"); xh2_stored = sem("xh2_stored"); xcT_psum = sem("xcT_psum"); xcT_ready = sem("xcT_ready")
        l_psum = sem("l_psum"); lc_ready = sem("lc_ready"); l_stored = sem("l_stored"); rm_ready = sem("rm_ready")
        ce_ready = sem("ce_ready"); cc_ready = sem("cc_ready"); lT_psum = sem("lT_psum"); cm_taken = sem("cm_taken")
        cT_psum = sem("cT_psum"); cT_stored = sem("cT_stored")
        diag_ready = sem("diag_ready"); cmb_psum = sem("cmb_psum"); cmb_stored = sem("cmb_stored")
        ds_ready = sem("ds_ready"); dexp_ready = sem("dexp_ready"); xs_psum = sem("xs_psum"); xsv_ready = sem("xsv_ready")
        xstd_ready = sem("xstd_ready"); xs_ready = sem("xs_ready"); xsT_psum = sem("xsT_psum"); xg_ready = sem("xg_ready")
        w_in = [sem(f"w_in{s}") for s in range(RING)]
        w_used = sem("w_used"); xgs_zero = sem("xgs_zero"); xgs_ready = sem("xgs_ready"); hs_ready = sem("hs_ready")
        hT_psum = sem("hT_psum"); hb_ready = sem("hb_ready"); h_ready = sem("h_ready"); ys_ready = sem("ys_ready")
        b2g_in = sem("b2g_in"); ctc_ready = sem("ctc_ready")
        part_psum = sem("part_psum"); part_added = sem("part_added"); out_done = sem("out_done")

        nodes = "(i p) d -> p i d"

        block = ctx.enter_context(nc.Block())

        @block.sync
        def _(sp):
            for v, a in ((SRCI, src), (DSTI, dst)):
                sp.dma_start(v, a.rearrange("(g p j) -> p g j", p=NP, j=ECH)).then_inc(edges_in, 16)
            for v, a in zip(AVEC, (a_src1, a_dst1)):
                sp.dma_start(v.rearrange("p f c -> p (f c)"), a.rearrange("h c -> (h c)")[None, :].to_broadcast([128, D])).then_inc(avec_in, 16)
            for k in range(KD):
                sp.dma_start(W1A[:, k, :, 0:HALF], W1[128 * k:128 * k + 128, :].rearrange("p (f c) -> p f c", f=2)).then_inc(w1_in, 16)
            for i in range(NT):
                sp.dma_start(X[:, i, :], x[NP * i:NP * i + NP, :]).then_inc(x_in, 16)
            sp.dma_start(B1R, b1[None, :].to_broadcast([NP, D])).then_inc(b1row_in, 16)
            sp.wait_ge(h1_psum, NT)
            for k in range(KD):
                sp.dma_start(W2A[:, k, :, 0:HALF], W2[128 * k:128 * k + 128, :].rearrange("p (f c) -> p f c", f=2)).then_inc(w2_in, 16)
            for v, a in zip(AVEC, (a_src2, a_dst2)):
                sp.dma_start(v.rearrange("p f c -> p (f c)"), a[0:1, :].to_broadcast([128, D])).then_inc(avec2_in, 16)
            with sp.Fori(0, NT // 2) as t:
                for s in range(2):
                    sp.wait_ge(neg_ready, t * 2 + (s + 1) + 1)
                    sp.dma_start(neg_dram[bass.ds(t * 2 + s, 1)].rearrange("o p n -> p (o n)"), NEGS[:, bass.ds(t * 2 + s, 1), :].rearrange("p o n -> p (o n)")).then_inc(neg_saved, 16)
            sp.wait_ge(neg_saved, 16 * NT)
            with sp.Fori(0, NT) as i:
                sp.wait_ge(masked, i * HEADS + 1)
                sp.dma_start(NEGC, neg_dram[bass.ds(i, 1)].rearrange("o p n -> p (o n)")).then_inc(neg_in, 16)
            sp.wait_ge(masked, NT * HEADS + 1)
            sp.dma_start(NEGC, neg_dram[0]).then_inc(neg2_in, 16)
            sp.wait_ge(o_psum, NT * HEADS + 2)
            for i in range(NT):
                sp.dma_start(X2[:, i, :], x[NP * i:NP * i + NP, :]).then_inc(x_again, 16)
            sp.dma_start(PHR, phi.rearrange("n p d -> (n p) d").rearrange("(t q) d -> q t d", q=128)).then_inc(phi_in, 16)
            sp.wait_ge(o1_ready, NT + 1)
            sp.dma_start(B2R, b2[None, :].to_broadcast([NP, D])).then_inc(b2row_in, 16)
            with sp.Fori(1, NT) as i:
                sp.wait_ge(masked2, i)
                sp.dma_start(NEGC, neg_dram[bass.ds(i, 1)].rearrange("o p n -> p (o n)")).then_inc(neg2_in, 16)
            sp.wait_ge(x2_ready, NT + 2)
            for v, a in zip(LDP, (ln_g, ln_b)):
                sp.dma_start(v, a).then_inc(par_in, 16)
            sp.dma_start(LDB, fb1).then_inc(par_in, 16)

            def fetch(weights, g, phase):
                for u in range(USES):
                    k, b, slot = u // SUB, u % SUB, u % RING
                    sp.wait_ge(w_used, phase * USES + (u + 1))
                    for q in range(0, QUAD, 2):
                        e = g * GE + (SUB * q + b)
                        if weights is w1:
                            rows = w1[bass.ds(e, 2, step=SUB), 128 * k:128 * k + 128, :].rearrange("q p h -> p q h")
                        else:
                            rows = w2[bass.ds(e, 2, step=SUB), 256 * k:256 * k + 256, :].rearrange("q (p j) d -> p q (j d)", j=2)
                        sp.dma_start(RG[slot][:, q:q + 2, :], rows).then_inc(w_in[slot], 16)

            def fetch_b2(g):
                sp.wait_ge(ys_ready, g + 1)
                for e in range(GE):
                    sp.dma_start(B2G[PSLOT * e:PSLOT * e + PSLOT, :], fb2[bass.ds(g * GE + e, 1), :].to_broadcast([PSLOT, D])).then_inc(b2g_in, 16)

            with sp.Fori(0, 1) as t:
                fetch(w1, t, t)
            with sp.Fori(0, ST - 1) as t:
                fetch(w1, t + 1, t * 2 + 1)
                fetch_b2(t)
                fetch(w2, t, t * 2 + 2)
            with sp.Fori(ST - 1, ST) as t:
                fetch_b2(t)
                fetch(w2, t, t * 2 + 1)
            for i in range(NT):
                sp.wait_ge(part_added, 2 * NT * (ST - 1) + 2 * i + 2 + NPB)
                sp.dma_start(out[NP * i:NP * i + NP, :], X2[:, i, :]).then_inc(out_done, 16)
            sp.wait_ge(out_done, 16 * NT)


        @block.gpsimd
        def _(pool):
            g = nc.gpsimd
            c = Chain(pool, pool_c)
            c.step(g.memset(IDENT, 0.0))
            g.affine_select(out=IDENT, in_=IDENT, compare_op=ALU.not_equal, fill=1.0, base=0,
                            pattern=[[-1, 128]], channel_multiplier=1).then_inc(ident_ready, 1)
            g.iota(IOI, pattern=[[1, NT * WIN]], base=1, channel_multiplier=0).then_inc(iota_ready, 1)
            g.memset(at(CNT_OFF, NT * (NODES + WIN) // 2, parts=NP), 0.0).then_inc(cnt_zero, 1)
            pool.wait_ge(span_ready, 2)
            g.partition_all_reduce(GAR.rearrange("p a b -> p (a b)"), GST.rearrange("p a b -> p (a b)"), NP, RMAX).then_inc(span_all, 1)
            pool.wait_ge(wa_ready, 2 * KD)
            g.memset(H1[:, :, :, HC:HC + 1], 1.0).then_inc(h1_ones, 1)
            pool.sem_inc(summed, 2)
            with pool.Fori(0, NT) as i:
                for h in range(HEADS):
                    pool.wait_ge(upper_ready, i * HEADS + (h + 1))
                    g.tensor_tensor(TR[h % 4], TR[h % 4], TS[h % 2], ALU.add).then_inc(summed, 1)
            pool.wait_ge(h2_stored, NT + 1)
            g.memset(H2[:, :, D:D + 1], 1.0).then_inc(h2_ones, 1)
            pool.wait_ge(x_again, 16 * NT)
            pool.wait_ge(b2row_in, 16)
            for i in range(NT):
                g.tensor_tensor(X2[:, i, :], X2[:, i, :], B2R, ALU.add).then_inc(xb_ready, 1)
                if i == 0:
                    pool.sem_inc(summed2, 2)
            with pool.Fori(0, NT // 2) as t:
                for s in range(2):
                    pool.wait_ge(upper2_ready, t * 2 + (s + 1))
                    g.tensor_tensor(TR[s], TR[s], TS[s], ALU.add).then_inc(summed2, 1)
            pool.wait_ge(phT_psum, ST)
            pool.wait_ge(x2_ready, NT + 2)
            g.memset(ONES, 1.0).then_inc(ones_ready, 1)
            g.memset(XH2[:, :, D:D + 1], 1.0).then_inc(ones_ready, 1)
            pool.sem_inc(xh2_stored, 2)
            pool.sem_inc(l_stored, 2)
            with pool.Fori(0, NT // 2) as t:
                for s in range(2):
                    pool.wait_ge(xc_ready, t * 2 + (s + 1))
                    g.tensor_copy(XH2[:, bass.ds(t * 2 + s, 1), 0:D].rearrange("p o d -> p (o d)"), XC[s]).then_inc(xh2_stored, 1)
                for s in range(2):
                    pool.wait_ge(lc_ready, t * 2 + (s + 3))
                    g.tensor_copy(L[:, bass.ds(t * 2 + s, 1), :].rearrange("p o d -> p (o d)"), LC[s]).then_inc(l_stored, 1)
            pool.wait_ge(xg_ready, ST + 1)
            pool.wait_ge(cT_stored, NT + 1)
            for v in (XGS, HTS):
                g.memset(v.rearrange("p k q c -> p (k q) c")[:, :, PSLOT:2 * PSLOT], 0.0).then_inc(xgs_zero, 1)

            def spaced(i):
                for b in range(SUB):
                    g.tensor_copy(XGS[:, :, :, 2 * PSLOT * b:2 * PSLOT * b + PSLOT],
                                  XGT[:, :, bass.ds(i * 128, 128)].rearrange("p k (q b r) -> p k q b r", b=SUB, r=PSLOT)[:, :, :, b, :]).then_inc(xgs_ready, 1)

            def weights(i):
                g.tensor_copy(CTC, CT[:, bass.ds(i, 1), :].rearrange("p o n -> p (o n)")).then_inc(ctc_ready, 1)

            spaced(0)
            weights(0)
            pool.wait_ge(w_used, w1_done(0))
            spaced(1)
            with pool.Fori(2, ST) as i:
                pool.wait_ge(w_used, (i - 1) * (2 * USES) + RING)
                spaced(i)
                pool.wait_ge(part_psum, (i - 1) * (2 * NT) + 1)
                weights(i - 1)
            pool.wait_ge(part_psum, (ST - 1) * (2 * NT) + 1)
            weights(ST - 1)


        @block.scalar
        def _(act):
            a = nc.scalar
            c = Chain(act, act_c)
            for free in (als_stored, h1_stored, h2_stored):
                act.sem_inc(free, 1)
            act.wait_ge(var_ready, 1)
            a.activation(STD, STD, ACT.Sqrt).then_inc(std_ready, 1)
            with act.Fori(0, NT // 2) as t:
                for s in range(2):
                    act.wait_ge(xT_psum, t * 2 + (s + 1) + 1)
                    a.copy(XT[s][:, 0:3, :], ps[:, 2 * s, 0:375].rearrange("p (a b) -> p a b", b=NP))
                    a.copy(XT[s][:, 3:6, :], ps[:, 2 * s + 1, 0:375].rearrange("p (a b) -> p a b", b=NP)).then_inc(xT_ready, 1)
                for s in range(2):
                    act.wait_ge(h1_psum, t * 2 + (s + 1))
                    act.wait_ge(h1_ones, 1)
                    for f in range(2):
                        a.copy(H1[:, bass.ds(t * 2 + s, 1), 4 * f:4 * f + 4, 0:HC].rearrange("p o h c -> p (o h) c"),
                               ps[0:NP, 4 + 2 * s + f, 0:HALF].rearrange("p (h c) -> p h c", c=HC))
                    a.copy(ALD[:, bass.ds(t * 2 + s, 1), :].rearrange("p o h -> p (o h)"), ps[0:NP, 5 + 2 * s, HALF:HALF + 8])
                    a.copy(ALSN[s], ps[0:NP, 4 + 2 * s, HALF:HALF + 8]).then_inc(h1_stored, 1)
                for s in range(2):
                    act.wait_ge(als_psum, t * 2 + (s + 1))
                    a.copy(ALS[:, :, bass.ds((t * 2 + s) * NP, NP)],
                           ps[0:NP, 2 * s:2 * s + 2, :].rearrange("p a (b n) -> p (a b) n", n=128)[:, :, 0:NP]).then_inc(als_stored, 1)
            act.wait_ge(cnt_done, 1)
            with act.Fori(0, NT // 2) as t:
                for s in range(2):
                    act.wait_ge(cntT_psum, t * 2 + 1)
                    a.copy(CF[s], CNT3[:, :, bass.ds((t * 2 + s) * NP, NP)]).then_inc(cnt_tile, 1)
            act.wait_ge(ald_scaled, 1)
            act.wait_ge(neg_saved, 16 * NT)
            with act.Fori(0, NT) as i:

                def upper(h):
                    act.wait_ge(masked, i * HEADS + (h + 1) + 1)
                    act.wait_ge(summed, i * HEADS + (h + 1))
                    a.activation(TS[h % 2], TR[h % 4], ACT.Relu, scale=(1 - SLOPE) / SLOPE,
                                 bias=ALU8[:, bass.ds(i, 1), h:h + 1].rearrange("p a b -> p (a b)")).then_inc(upper_ready, 1)

                upper(0)
                for h in range(HEADS):
                    if h + 1 < HEADS:
                        upper(h + 1)
                    act.wait_ge(shift_ready, i * HEADS + (h + 1))
                    act.wait_ge(summed, i * HEADS + (h + 3))
                    a.activation(TR[h % 4], TR[h % 4], ACT.Exp, bias=NL[:, h:h + 1]).then_inc(e_ready, 1)
                act.wait_ge(elu_in, i + 1)
                a.activation(EL, EL, ACT.Exp).then_inc(elu_exp, 1)
                act.wait_ge(o1T_psum, i + 1)
                for f in range(2):
                    last = a.copy(O1T[:, 3 * f:3 * f + 3, :], ps[:, f, 0:375].rearrange("p (a b) -> p a b", b=NP))
                last.then_inc(o1T_ready, 1)
                act.wait_ge(h2_psum, i + 1)
                for f in range(2):
                    a.copy(H2[:, bass.ds(i, 1), f * HALF:f * HALF + HALF].rearrange("p o d -> p (o d)"), ps[0:NP, 3 + f, 0:HALF])
                a.copy(ALD2[:, bass.ds(i, 1)], ps[0:NP, 4, HALF:HALF + 1])
                a.copy(ALS2N[:, bass.ds(i, 1)], ps[0:NP, 3, HALF:HALF + 1]).then_inc(h2_stored, 1)
            act.wait_ge(als2_psum, 1)
            a.copy(ALS2.rearrange("p (a n) -> p a n", n=NP), PST(0, NT, 0)[0:NP]).then_inc(als2_stored, 1)
            act.wait_ge(ald2_scaled, 1)
            with act.Fori(0, NT // 2) as t:
                for s in range(2):
                    i = t * 2 + s
                    act.wait_ge(masked2, t * 2 + (s + 1))
                    act.wait_ge(summed2, t * 2 + (s + 1))
                    a.activation(TS[s], TR[s], ACT.Relu, scale=(1 - SLOPE) / SLOPE, bias=ALU8B[:, bass.ds(i, 1)]).then_inc(upper2_ready, 1)
                for s in range(2):
                    act.wait_ge(shift2_ready, t * 2 + (s + 1))
                    act.wait_ge(summed2, t * 2 + (s + 3))
                    a.activation(TR[s], TR[s], ACT.Exp, bias=NL[:, s:s + 1]).then_inc(e2_ready, 1)
            act.wait_ge(var2_ready, 1)
            a.activation(STD, STD, ACT.Sqrt).then_inc(std2_ready, 1)
            for s in range(ST):
                act.wait_ge(phT_psum, s + 1)
                a.copy(PHT[:, :, 128 * s:128 * s + 128], PSW(2 * (s % 2), KD)).then_inc(phT_stored, 1)
            act.wait_ge(par_psum, 1)
            for q, w in enumerate((GT, BT)):
                a.copy(w, ps[:, 4 + q, 0:KD * NEXP].rearrange("p (k n) -> p k n", n=NEXP))
            act.wait_ge(par_psum, 2)
            a.copy(FB1T[:, 0:8, :], ps[:, 0, :].rearrange("p (k n) -> p k n", n=NEXP))
            a.copy(FB1T[:, 8:12, :], ps[:, 1, 0:4 * NEXP].rearrange("p (k n) -> p k n", n=NEXP)).then_inc(par_stored, 1)
            act.wait_ge(nrm_ready, 1)
            a.activation(NRM, NRM, ACT.Sqrt).then_inc(nrs_ready, 1)
            act.sem_inc(xcT_ready, 1)
            act.sem_inc(lc_ready, 2)
            act.sem_inc(cT_stored, 1)
            with act.Fori(0, NT // 2) as t:
                for s in range(2):
                    act.wait_ge(xcT_psum, t * 2 + (s + 3))
                    for f in range(2):
                        last = a.copy(XCT[s][:, 3 * f:3 * f + 3, :], ps[:, f, 0:375].rearrange("p (a b) -> p a b", b=NP))
                    last.then_inc(xcT_ready, 1)
                for s in range(2):
                    act.wait_ge(l_psum, t * 2 + (s + 1))
                    act.wait_ge(l_stored, t * 2 + (s + 1))
                    act.wait_ge(lT_psum, t * 2 + (s + 1))
                    a.copy(LC[s].rearrange("p (a n) -> p a n", n=512), ps[0:NP, 2 + 2 * s:4 + 2 * s, :]).then_inc(lc_ready, 1)
                    act.wait_ge(rm_ready, t * 2 + (s + 1))
                    act.wait_ge(cT_psum, t * 2 + (s + 1))
                    a.activation(CC[s], LC[s], ACT.Exp, bias=RM[s], accum_out=RS[s]).then_inc(ce_ready, 1)
                for s in range(2):
                    act.wait_ge(cT_psum, t * 2 + (s + 3))
                    a.copy(CT[:, :, bass.ds((t * 2 + s) * NP, NP)], PSW(6, ST, NP)).then_inc(cT_stored, 1)
            act.wait_ge(cmb_psum, 1)
            a.copy(CMB.rearrange("p (a n) -> p a n", n=512), ps[0:NP, 4:6, :]).then_inc(cmb_stored, 1)

            def disp(s, p):
                act.wait_ge(ds_ready, s + 1)
                a.activation(DC[p], DC[p], ACT.Exp).then_inc(dexp_ready, 1)

            def spread(s):
                act.wait_ge(xsv_ready, s + 1)
                a.activation(SSD, SSD, ACT.Sqrt).then_inc(xstd_ready, 1)

            def body(t, more):
                disp(2 * t + 1, 1)
                spread(2 * t)
                if more:
                    disp(2 * t + 2, 0)
                spread(2 * t + 1)

            disp(0, 0)
            with act.Fori(0, ST // 2 - 1) as t:
                body(t, True)
            body(ST // 2 - 1, False)
            act.wait_ge(xgs_zero, 2)
            act.sem_inc(hs_ready, 1)
            act.sem_inc(h_ready, 1)

            def hidden(g):
                act.wait_ge(w_used, w1_done(g))
                act.wait_ge(hT_psum, g + 1)
                a.copy(HS.rearrange("p (j n) -> p j n", n=512), ps[:, 0:3, :]).then_inc(hs_ready, 1)
                act.wait_ge(hb_ready, g + 2)
                if not isinstance(g, int):
                    act.wait_ge(w_used, g * (2 * USES) + (RING + USES))
                for b in range(SUB):
                    last = a.activation(HTS.rearrange("p k q c -> p (k q) c")[:, :, 2 * PSLOT * b:2 * PSLOT * b + PSLOT],
                                        HB.rearrange("p k (q b r) -> p (k q) b r", b=SUB, r=PSLOT)[:, :, b, :], ACT.Gelu)
                last.then_inc(h_ready, 1)

            hidden(0)
            with act.Fori(1, ST) as g:
                hidden(g)


        @block.vector
        def _(dve):
            v = nc.vector
            c = Chain(dve, dve_c)
            for free in (masked, group_added, o1_ready, neg_ready):
                dve.sem_inc(free, 1)
            dve.wait_ge(edges_in, 32)
            c.step(v.tensor_copy(SRCF, SRCI.rearrange("p g j -> p (g j)")))
            c.step(v.tensor_copy(DSTF, DSTI))
            v.tensor_reduce(GST[:, 1, :], DSTF, AX_X, ALU.max).then_inc(span_ready, 1)
            c.step(v.tensor_reduce(GST[:, 0, :], DSTF, AX_X, ALU.min))
            v.tensor_scalar(GST[:, 0, :], GST[:, 0, :], -1.0, None, ALU.mult).then_inc(span_ready, 1)
            c.step(v.tensor_scalar(TA, SRCF, float(NP), None, ALU.is_ge))
            for k in range(2, NT):
                c.step(v.scalar_tensor_tensor(out=TA, in0=SRCF, scalar=float(NP * k), in1=TA, op0=ALU.is_ge, op1=ALU.add))
            c.step(v.scalar_tensor_tensor(out=KEYB, in0=TA, scalar=-float(NP), in1=SRCF, op0=ALU.mult, op1=ALU.add))
            c.step(v.tensor_scalar(KEYA.rearrange("p g j -> p (g j)"), TA, float(WIN), 1.0, ALU.mult, ALU.add))
            dve.wait_ge(iota_ready, 1)
            c.step(v.tensor_copy(IOK, IOI))
            c.step(v.tensor_scalar(IOB, IOI[:, 0:128], -1.0, None, ALU.add))
            dve.wait_ge(span_all, 1)
            c.step(v.tensor_tensor(SPAN, GAR[:, 0, :], GAR[:, 1, :], ALU.add))
            c.step(v.tensor_reduce(FLG[:, 0:1], SPAN, AX_X, ALU.max))
            c.step(v.tensor_scalar(FLG[:, 1:2], FLG[:, 0:1], WIN - 0.5, None, ALU.is_lt))
            c.step(v.tensor_scalar(WPI, FLG[:, 1:2], 1.0 - NWIN, float(NWIN), ALU.mult, ALU.add))
            v.tensor_scalar(D0, GAR[:, 0, :], -1.0, FLG[:, 1:2], ALU.mult, ALU.mult).then_inc(windows_ready, 1)
            dve.wait_ge(avec_in, 32)
            dve.wait_ge(w1_in, 16 * KD)
            for k in range(KD):
                for q in range(2):
                    c.step(v.tensor_tensor(AW[q], W1A[:, k, :, 0:HALF], AVEC[q], ALU.mult))
                    v.tensor_reduce(W1A[:, k, q, HALF:HALF + HEADS], AW[q].rearrange("p f (h c) -> p (f h) c", c=HC),
                                    AX_X, ALU.add).then_inc(wa_ready, 1)
                dve.wait_ge(wa_ready, 2 * k + 2)
            dve.wait_ge(x_in, 16 * NT)
            for i in range(NT):
                for f in range(2):
                    c.step(v.bn_stats(BST[:, i, f, :], X[:, i, f * HALF:f * HALF + HALF]))
                c.step(v.bn_aggr(MV[:, i, :], BST[:, i, :, :].rearrange("p f s -> p (f s)")))
            v.tensor_scalar(STD, MV[:, :, 1], EPS_LN, None, ALU.add).then_inc(var_ready, 1)
            dve.wait_ge(std_ready, 1)
            c.step(v.reciprocal(RSTD, STD))
            with dve.Fori(0, NT // 2) as t:
                for s in range(2):
                    dve.wait_ge(xT_psum, t * 2 + 1)
                    v.tensor_scalar(XH[s], X[:, bass.ds(t * 2 + s, 1), :].rearrange("p o d -> p (o d)"),
                                    MV[:, bass.ds(t * 2 + s, 1), 0:1].rearrange("p a b -> p (a b)"), RSTD[:, bass.ds(t * 2 + s, 1)],
                                    ALU.subtract, ALU.mult).then_inc(xhat_ready, 1)

            dve.wait_ge(windows_ready, 1)
            nwin = v.value_load(WPI[0:1, 0:1], min_val=1, max_val=NWIN)
            c = Chain(dve, count_c)
            with dve.Fori(0, nwin) as w:
                c.enter(w, 6)
                c.step(v.tensor_copy(D0I, D0))
                c.step(v.tensor_tensor(TD, DSTF, D0[:, :].unsqueeze(2).to_broadcast([NP, NGROUP, ECH]), ALU.subtract))
                c.step(v.tensor_scalar(MK, TD, -0.5, None, ALU.is_gt))
                c.step(v.scalar_tensor_tensor(out=MK, in0=TD, scalar=WIN - 0.5, in1=MK, op0=ALU.is_lt, op1=ALU.mult))
                c.step(v.tensor_tensor(TD, TD, KEYA, ALU.add))
                v.tensor_scalar(D0, D0, float(WIN), None, ALU.add).then_inc(windows_ready, 1)
                dve.wait_ge(windows_ready, w + 2)
                dve.wait_ge(group_added, w * NGROUP + 1)
                dve.wait_ge(cnt_zero, 1)
                c.step(v.tensor_tensor(KEY, TD, MK, ALU.mult))
                dve.sem_inc(keys_known, 1)
                with dve.Fori(0, NGROUP // 2) as t:
                    for s in range(2):
                        for j in range(ECH):
                            r = j % OHR
                            n = (w * NGROUP + t * 2 + s) * ECH + j
                            dve.wait_ge(chunk_counted, n + 1)
                            v.tensor_scalar(OB[r][:, 0:NP], IOB[:, 0:NP], KEYB[:, bass.ds((t * 2 + s) * ECH + j, 1)], None, ALU.is_equal)
                            v.tensor_scalar(OK[r], IOK, KEY[:, bass.ds(t * 2 + s, 1), j:j + 1].rearrange("p a b -> p (a b)"), None,
                                            ALU.is_equal).then_inc(onehot_ready, 1)
                    for s in range(2):
                        dve.wait_ge(chunk_counted, (w * NGROUP + t * 2 + s + 1) * ECH + OHR)
                        d0 = v.value_load(D0I[0:1, bass.ds(t * 2 + s, 1)], min_val=0, max_val=NODES - 1)
                        win = CNT3[:, :, bass.ds(d0, WIN)]
                        v.tensor_tensor(win, ps[0:NP, s, 0:NT * WIN].rearrange("p (a b) -> p a b", b=WIN), win, ALU.add).then_inc(group_added, 1)
                        dve.wait_ge(group_added, w * NGROUP + t * 2 + s + 1 + 1)
            c = Chain(dve, attend_c)
            v.memset(FLG[:, 0:1], 0.0).then_inc(cnt_done, 1)
            with dve.Fori(0, NT // 2) as t:
                for s in range(2):
                    dve.wait_ge(cntT_psum, t * 2 + s + 1 + 1)
                    v.tensor_scalar(NEGS[:, bass.ds(t * 2 + s, 1), :].rearrange("p o (a n) -> p (o a) n", n=NP), PST(0, NT, 4 * s)[0:NP], 0.5, NO_EDGE, ALU.is_lt, ALU.mult).then_inc(neg_ready, 1)
            dve.wait_ge(w2_in, 16 * KD)
            dve.wait_ge(avec2_in, 32)
            dve.wait_ge(cntT_psum, NT + 1)
            for k in range(KD):
                for q in range(2):
                    c.step(v.tensor_tensor(AW2[q], W2A[:, k, :, 0:HALF], AVEC[q], ALU.mult))
                    v.tensor_reduce(W2A[:, k, q, HALF:HALF + 1], AW2[q], mybir.AxisListType.XY, ALU.add).then_inc(wa2_ready, 1)
                dve.wait_ge(wa2_ready, 2 * k + 2)

            dve.wait_ge(b1row_in, 16)
            dve.wait_ge(neg_saved, 16 * NT)
            dve.wait_ge(als_stored, NT + 1)
            dve.wait_ge(h1_stored, NT + 1)

            def shift(al, j, done):
                c.step(v.tensor_scalar(TN[:, j:j + 1], M0[:, j:j + 1], 1 / SLOPE, al, ALU.mult, ALU.add))
                c.step(v.scalar_tensor_tensor(out=NM[:, j:j + 1], in0=TN[:, j:j + 1], scalar=SLOPE, in1=TN[:, j:j + 1],
                                              op0=ALU.mult, op1=ALU.max))
                v.scalar_tensor_tensor(out=NL[:, j:j + 1], in0=al, scalar=SLOPE, in1=NM[:, j:j + 1],
                                       op0=ALU.mult, op1=ALU.subtract).then_inc(done, 1)

            v.tensor_scalar(ALU8, ALD, 1 - SLOPE, None, ALU.mult).then_inc(ald_scaled, 1)
            with dve.Fori(0, NT) as i:
                c.enter(i, L1_STEPS)

                def mask(h):
                    if h == 0:
                        dve.wait_ge(neg_in, i * 16 + 16)
                    dve.wait_ge(eT_psum, i * HEADS + (h + 1))
                    dve.sem_inc(slot_taken, 1)
                    v.tensor_tensor_reduce(out=TR[h % 4], in0=NEGC, in1=ALS[:, h, :], scale=SLOPE, scalar=MAX_FLOOR,
                                           op0=ALU.add, op1=ALU.max, accum_out=M0[:, h:h + 1]).then_inc(masked, 1)
                    dve.wait_ge(masked, i * HEADS + (h + 1) + 1)
                    shift(ALD[:, bass.ds(i, 1), h:h + 1].rearrange("p a b -> p (a b)"), h, shift_ready)

                mask(0)
                mask(1)
                mask(2)
                for h in range(HEADS):
                    if h + 3 < HEADS:
                        mask(h + 3)
                    dve.wait_ge(eT_psum, i * HEADS + (h + 5))
                    dve.wait_ge(o_psum, i * HEADS + (h + 1))
                    v.tensor_tensor(PR[h % 2], PST(0, NT, 3 * (h % 2))[0:NP], CNT3[:, :, bass.ds(i * NP, NP)], ALU.mult).then_inc(p_ready, 1)
                dve.wait_ge(o_psum, i * HEADS + (HEADS + 2))
                for f in range(2):
                    q = ps[0:NP, 6 + f, 0:4 * (HC + 1)].rearrange("p (h c) -> p h c", c=HC + 1)
                    c.step(v.tensor_scalar(RZ[:, 4 * f:4 * f + 4], q[:, :, HC:HC + 1].rearrange("p h c -> p (h c)"), EPS_Z, None, ALU.add))
                c.step(v.reciprocal(RZ, RZ))
                for f in range(2):
                    q = ps[0:NP, 6 + f, 0:4 * (HC + 1)].rearrange("p (h c) -> p h c", c=HC + 1)
                    last = v.tensor_tensor(O1[:, f * HALF:f * HALF + HALF].rearrange("p (h c) -> p h c", c=HC), q[:, :, 0:HC],
                                           RZ[:, 4 * f:4 * f + 4].unsqueeze(2).to_broadcast([NP, 4, HC]), ALU.mult)
                    c.step(last)
                c.step(v.tensor_tensor(O1, O1, B1R, ALU.add))
                v.tensor_scalar(EL, O1, 0.0, None, ALU.min).then_inc(elu_in, 1)
                dve.wait_ge(elu_exp, i + 1)
                c.step(v.tensor_scalar(EL, EL, -1.0, None, ALU.add))
                v.scalar_tensor_tensor(out=O1, in0=O1, scalar=0.0, in1=EL, op0=ALU.max, op1=ALU.add).then_inc(o1_ready, 1)
            c.leave(NT)
            c = Chain(dve, second_c)
            dve.wait_ge(h2_stored, NT + 1)
            v.tensor_scalar(ALU8B, ALD2, 1 - SLOPE, None, ALU.mult).then_inc(ald2_scaled, 1)

            def mask2(i, s):
                dve.wait_ge(neg2_in, i * 16 + 16)
                dve.wait_ge(als2_stored, 1)
                dve.sem_inc(slot_taken, 1)
                v.tensor_tensor_reduce(out=TR[s], in0=NEGC, in1=ALS2, scale=SLOPE, scalar=MAX_FLOOR,
                                       op0=ALU.add, op1=ALU.max, accum_out=M0[:, s:s + 1]).then_inc(masked2, 1)
                dve.wait_ge(masked2, i + 1)
                shift(ALD2[:, bass.ds(i, 1)], s, shift2_ready)

            def weights2(i, s):
                dve.wait_ge(eT2_psum, i + 1)
                v.tensor_tensor(PR[s], PST(0, NT, 0)[0:NP], CNT3[:, :, bass.ds(i * NP, NP)], ALU.mult).then_inc(p2_ready, 1)

            def finish2(i, s):
                dve.wait_ge(o2_psum, i + 1)
                c.step(v.tensor_scalar(RZ[:, s:s + 1], ps[0:NP, 4 + 2 * s, HALF:HALF + 1], EPS_Z, None, ALU.add))
                c.step(v.reciprocal(RZ[:, s:s + 1], RZ[:, s:s + 1]))
                xi = X2[:, bass.ds(i, 1), :].rearrange("p o (f d) -> p (o f) d", f=2)
                c.step(v.scalar_tensor_tensor(out=xi, in0=ps[0:NP, 3 + 2 * s:5 + 2 * s, 0:HALF], scalar=RZ[:, s:s + 1], in1=xi,
                                              op0=ALU.mult, op1=ALU.add))
                for f in range(2):
                    dve.sem_inc(slot_taken, 1)
                    c.step(v.bn_stats(BS2[:, f, :], xi[:, f, :]))
                dve.sem_inc(slot_taken, 1)
                c.step(v.bn_aggr(MV1, BS2.rearrange("p f s -> p (f s)")))
                v.tensor_copy(MV[:, bass.ds(i, 1), :].rearrange("p o a -> p (o a)"), MV1).then_inc(x2_ready, 1)

            def body2(t, i, more):
                c.enter(t, 2 * 6 + (2 * 2 if more else 0))
                for s in range(2):
                    weights2(i + s, s)
                for s in range(2):
                    if more:
                        mask2(i + (2 + s), s)
                for s in range(2):
                    finish2(i + s, s)

            for s in range(2):
                mask2(s, s)
            dve.wait_ge(xb_ready, NT)
            with dve.Fori(0, NT // 2 - 1) as t:
                body2(t, t * 2, True)
            c.leave(NT // 2 - 1)
            c = Chain(dve, expert_c)
            body2(0, NT - 2, False)
            c.leave(1)
            dve.wait_ge(x2_ready, NT + 2)
            v.tensor_scalar(STD, MV[:, :, 1], EPS_LN, None, ALU.add).then_inc(var2_ready, 1)
            dve.wait_ge(std2_ready, 1)
            c.step(v.reciprocal(RSTD, STD))
            dve.wait_ge(phT_stored, ST)
            for k in range(KD):
                c.step(v.tensor_tensor(SQ[k % 2], PHT[:, k, :], PHT[:, k, :], ALU.mult))
                c.step(v.tensor_reduce(NRM[:, k, :], SQ[k % 2].rearrange("p (n q) -> p q n", q=PSLOT), AX_X, ALU.add))
            v.tensor_scalar(NRM, NRM, EPS_PHI, None, ALU.add).then_inc(nrm_ready, 1)
            dve.wait_ge(nrs_ready, 1)
            c.step(v.reciprocal(NRR, NRM))
            for k in range(KD):
                kv = PHT[:, k, :].rearrange("p (n q) -> p n q", q=PSLOT)
                v.tensor_tensor(kv, kv, NRR[:, k:k + 1, :].to_broadcast([128, NEXP, PSLOT]), ALU.mult).then_inc(phn_ready, 1)
            dve.wait_ge(phn_ready, KD)
            dve.wait_ge(par_psum, 2)
            c = Chain(dve, logit_c)
            with dve.Fori(0, NT // 2) as t:
                c.enter(t, 2 + 2)
                for s in range(2):
                    i = t * 2 + s
                    dve.wait_ge(xcT_psum, t * 2 + (s + 1))
                    dve.wait_ge(xh2_stored, t * 2 + (s + 1))
                    v.tensor_scalar(XC[s], X2[:, bass.ds(i, 1), :].rearrange("p o d -> p (o d)"),
                                    MV[:, bass.ds(i, 1), 0:1].rearrange("p a b -> p (a b)"), RSTD[:, bass.ds(i, 1)],
                                    ALU.subtract, ALU.mult).then_inc(xc_ready, 1)
                for s in range(2):
                    dve.wait_ge(lc_ready, t * 2 + (s + 3))
                    c.step(v.tensor_reduce(RM[s], LC[s], AX_X, ALU.max))
                    v.tensor_scalar(RM[s], RM[s], -1.0, None, ALU.mult).then_inc(rm_ready, 1)
                    dve.wait_ge(ce_ready, t * 2 + (s + 1))
                    c.step(v.reciprocal(RI[s], RS[s]))
                    v.tensor_scalar(CC[s], CC[s], RI[s], None, ALU.mult).then_inc(cc_ready, 1)
                for s in range(2):
                    dve.wait_ge(lT_psum, t * 2 + (s + 3))
                    v.tensor_reduce(CMX[:, :, bass.ds(t * 2 + s, 1)].rearrange("p a o -> p (a o)"), PSW(6, ST, NP), AX_X, ALU.max).then_inc(cm_taken, 1)
            c.leave(NT // 2)
            dve.wait_ge(cm_taken, NT)
            c.step(v.tensor_reduce(CMN, CMX, AX_X, ALU.max))
            c.step(v.tensor_scalar(CMN, CMN, -1.0, None, ALU.mult))
            dve.wait_ge(lT_psum, NT + 2)
            dve.wait_ge(l_stored, NT + 2)
            v.tensor_tensor(DIAG, IDENT.unsqueeze(1).to_broadcast([128, ST, 128]), CMN.unsqueeze(2).to_broadcast([128, ST, 128]),
                            ALU.mult).then_inc(diag_ready, 1)
            dve.wait_ge(cmb_stored, 1)

            def less(s, p):
                dve.wait_ge(xs_psum, s + 1)
                v.tensor_tensor(DC[p], L[:, :, bass.ds(s * 128, 128)],
                                CMB[:, bass.ds(s * 128, 128)].unsqueeze(1).to_broadcast([NP, NT, 128]), ALU.add).then_inc(ds_ready, 1)

            def inputs(s, p):
                o = ps[:, 2 * p:2 * p + 2, 0:HALF]
                dve.wait_ge(xs_psum, s + 3)
                c.step(v.reciprocal(CSI, ps[:, 2 * p + 1, HALF:HALF + 1]))
                dve.wait_ge(xsT_psum, s + 1)
                c.step(v.tensor_scalar(XSW.rearrange("p (f d) -> p f d", f=2), o, CSI, None, ALU.mult))
                for f in range(2):
                    dve.sem_inc(slot_taken, 1)
                    c.step(v.bn_stats(SST[:, f, :], XSW[:, f * HALF:f * HALF + HALF]))
                dve.sem_inc(slot_taken, 1)
                c.step(v.bn_aggr(SMV, SST.rearrange("p f s -> p (f s)")))
                v.tensor_scalar(SSD, SMV[:, 1:2], EPS_LN, None, ALU.add).then_inc(xsv_ready, 1)
                dve.wait_ge(xstd_ready, s + 1)
                c.step(v.reciprocal(SRD, SSD))
                v.tensor_scalar(XSW, XSW, SMV[:, 0:1], SRD, ALU.subtract, ALU.mult).then_inc(xs_ready, 1)

            def gain(s, p):
                dve.wait_ge(xsT_psum, s + 2)
                xg = XGT[:, :, bass.ds(s * 128, 128)].rearrange("p k (n q) -> p k n q", q=PSLOT)
                c.step(v.tensor_tensor(xg, PSW(4 + 2 * p, KD).rearrange("p k (n q) -> p k n q", q=PSLOT),
                                       GT[:, :, bass.ds(s * GE, GE)].unsqueeze(3).to_broadcast([128, KD, GE, PSLOT]), ALU.mult))
                v.tensor_tensor(xg, xg, BT[:, :, bass.ds(s * GE, GE)].unsqueeze(3).to_broadcast([128, KD, GE, PSLOT]),
                                ALU.add).then_inc(xg_ready, 1)

            def body3(t, a, more):
                c.enter(t, 2 * 7)
                less(a + 1, 1)
                inputs(a, 0)
                gain(a, 0)
                if more:
                    less(a + 2, 0)
                inputs(a + 1, 1)
                gain(a + 1, 1)

            dve.wait_ge(par_stored, 1)
            less(0, 0)
            c = Chain(dve, input_c)
            with dve.Fori(0, ST // 2 - 1) as t:
                body3(t, t * 2, True)
            c.leave(ST // 2 - 1)
            body3(0, ST - 2, False)
            dve.wait_ge(xg_ready, ST + 1)
            dve.sem_inc(hb_ready, 1)
            dve.sem_inc(ys_ready, 1)
            dve.sem_inc(part_added, NPB)

            def hidden(g):
                dve.wait_ge(hT_psum, g + 2)
                dve.wait_ge(h_ready, g + 1)
                v.tensor_tensor(HB.rearrange("p k (e r) -> p k e r", r=PSLOT),
                                ps[:, 5:8, :].rearrange("p a (b e r) -> p (a b) e r", e=GE, r=PSLOT),
                                FB1T[:, :, bass.ds(g * GE, GE)].unsqueeze(3).to_broadcast([128, KH, GE, PSLOT]), ALU.add).then_inc(hb_ready, 1)

            def results(g):
                dve.wait_ge(w_used, w2_done(g))
                dve.wait_ge(b2g_in, g * (16 * GE) + 16 * GE)
                dve.wait_ge(part_psum, g * (2 * NT) + 1)
                v.tensor_tensor(YS.rearrange("p (f d) -> p f d", f=2), ps[:, 3:5, 0:HALF], B2G.rearrange("p (f d) -> p f d", f=2),
                                ALU.add).then_inc(ys_ready, 1)

            def onto(g):
                for n in range(2 * NT):
                    dve.wait_ge(part_psum, g * (2 * NT) + (n + 2))
                    xm = X2[:, n // 2, HALF * (n % 2):HALF * (n % 2) + HALF]
                    v.tensor_tensor(xm, ps[0:NP, 5 + n % NPB, 0:HALF], xm, ALU.add).then_inc(part_added, 1)

            with dve.Fori(0, 2) as t:
                hidden(t)
            with dve.Fori(0, ST - 2) as t:
                results(t)
                onto(t)
                hidden(t + 2)
            for g in range(ST - 2, ST):
                results(g)
                onto(g)


        @block.tensor
        def _(pe):
            m = nc.tensor
            for free in (xT_psum, cntT_psum):
                pe.sem_inc(free, 1)
            pe.wait_ge(ident_ready, 1)
            pe.wait_ge(wa_ready, 2 * KD)
            with pe.Fori(0, NT // 2) as t:
                for s in range(2):
                    pe.wait_ge(xhat_ready, t * 2 + (s + 1))
                    pe.wait_ge(als_stored, t * 2 + 1)
                    for k in range(KD):
                        last = m.transpose(ps[:, 2 * s + k // 3, NP * (k % 3):NP * (k % 3) + NP], XH[s][:, 128 * k:128 * k + 128], IDENT[0:NP, 0:NP])
                    last.then_inc(xT_psum, 1)
                for s in range(2):
                    pe.wait_ge(xT_ready, t * 2 + (s + 1))
                    pe.wait_ge(h1_stored, t * 2 + 1)
                    for f in range(2):
                        for k in range(KD):
                            last = m.matmul(ps[0:NP, 4 + 2 * s + f, 0:HALF + 8], XT[s][:, k, :], W1A[:, k, f, :], start=(k == 0), stop=(k == KD - 1))
                    last.then_inc(h1_psum, 1)
                for s in range(2):
                    pe.wait_ge(h1_stored, t * 2 + (s + 1) + 1)
                    for h in range(HEADS):
                        last = m.matmul(ps[0:NP, 2 * s + h // 4, 128 * (h % 4):128 * (h % 4) + NP], ALSN[s][:, h:h + 1].to_broadcast([NP, NP]),
                                        IDENT[0:NP, 0:NP], start=True, stop=True)
                    last.then_inc(als_psum, 1)
            pe.wait_ge(als_stored, NT + 1)
            pe.wait_ge(windows_ready, 1)
            pe.sem_inc(chunk_counted, OHR)
            nwin = m.value_load(WPI[0:1, 0:1], min_val=1, max_val=NWIN)
            with pe.Fori(0, nwin) as w:
                with pe.Fori(0, NGROUP // 2) as t:
                    for s in range(2):
                        pe.wait_ge(group_added, w * NGROUP + t * 2 + 1)
                        for j in range(ECH):
                            pe.wait_ge(onehot_ready, (w * NGROUP + t * 2 + s) * ECH + j + 1)
                            m.matmul(ps[0:NP, s, 0:NT * WIN], OB[j % OHR][:, 0:NP], OK[j % OHR], start=(j == 0), stop=(j == ECH - 1)).then_inc(chunk_counted, 1)
            with pe.Fori(0, NT // 2) as t:
                for s in range(2):
                    pe.wait_ge(cnt_tile, t * 2 + s + 1)
                    pe.wait_ge(neg_ready, t * 2 + 1)
                    for k in range(NT):
                        last = m.transpose(PST(k, 1, 4 * s)[0:NP, 0, :], CF[s][:, k, :], IDENT[0:NP, 0:NP])
                    last.then_inc(cntT_psum, 1)
            pe.wait_ge(neg_ready, NT + 1)
            pe.wait_ge(wa2_ready, 2 * KD)
            pe.sem_inc(eT_psum, 4)
            pe.sem_inc(o_psum, 2)
            with pe.Fori(0, NT) as i:

                def turn(h):
                    pe.wait_ge(e_ready, i * HEADS + (h + 1))
                    if h >= 2:
                        pe.wait_ge(p_ready, i * HEADS + (h - 1))
                    else:
                        pe.wait_ge(h2_stored, i + 1)
                    for k in range(NT):
                        last = m.transpose(PST(k, 1, 3 * (h % 2))[0:NP, 0, :], TR[h % 4][:, NP * k:NP * k + NP], IDENT[0:NP, 0:NP])
                    last.then_inc(eT_psum, 1)

                turn(0)
                for h in range(HEADS):
                    if h + 1 < HEADS:
                        turn(h + 1)
                    pe.wait_ge(p_ready, i * HEADS + (h + 1))
                    if h == 0:
                        pe.wait_ge(o1_ready, i + 1)
                    for k in range(NT):
                        last = m.matmul(ps[0:NP, 6 + h // 4, (HC + 1) * (h % 4):(HC + 1) * (h % 4) + HC + 1], PR[h % 2][:, k, :], H1[:, k, h, :],
                                        start=(k == 0), stop=(k == NT - 1))
                    last.then_inc(o_psum, 1)
                pe.wait_ge(o1_ready, i + 1 + 1)
                for k in range(KD):
                    last = m.transpose(ps[:, k // 3, NP * (k % 3):NP * (k % 3) + NP], O1[:, 128 * k:128 * k + 128], IDENT[0:NP, 0:NP])
                last.then_inc(o1T_psum, 1)
                pe.wait_ge(o1T_ready, i + 1)
                for f in range(2):
                    for k in range(KD):
                        last = m.matmul(ps[0:NP, 3 + f, 0:HALF + 1], O1T[:, k, :], W2A[:, k, f, :], start=(k == 0), stop=(k == KD - 1))
                last.then_inc(h2_psum, 1)
            pe.wait_ge(h2_stored, NT + 1)
            for i in range(NT):
                last = m.matmul(PST(i, 1, 0)[0:NP, 0, :], ALS2N[:, i:i + 1].to_broadcast([NP, NP]), IDENT[0:NP, 0:NP], start=True, stop=True)
            last.then_inc(als2_psum, 1)
            pe.wait_ge(als2_stored, 1)
            pe.wait_ge(h2_ones, 1)

            def turn2(i, s):
                pe.wait_ge(e2_ready, i + 1)
                pe.wait_ge(p2_ready, i + 1)
                for k in range(NT):
                    last = m.transpose(PST(k, 1, 0)[0:NP, 0, :], TR[s][:, NP * k:NP * k + NP], IDENT[0:NP, 0:NP])
                last.then_inc(eT2_psum, 1)

            def gather2(i, s):
                pe.wait_ge(p2_ready, i + 2)
                pe.wait_ge(x2_ready, i + 1)
                for f in range(2):
                    for k in range(NT):
                        last = m.matmul(ps[0:NP, 3 + 2 * s + f, 0:HALF + f], PR[s][:, k, :], H2[:, k, f * HALF:f * HALF + HALF + f],
                                        start=(k == 0), stop=(k == NT - 1))
                last.then_inc(o2_psum, 1)

            def body(i, more):
                turn2(i + 1, 1)
                gather2(i, 0)
                if more:
                    turn2(i + 2, 0)
                gather2(i + 1, 1)

            pe.sem_inc(p2_ready, 1)
            pe.sem_inc(x2_ready, 2)
            turn2(0, 0)
            with pe.Fori(0, NT // 2 - 1) as t:
                body(t * 2, True)
            body(NT - 2, False)
            pe.wait_ge(x2_ready, NT + 2)
            pe.wait_ge(phi_in, 16)
            for s in range(ST):
                if s >= 2:
                    pe.wait_ge(phT_stored, s - 1)
                for k in range(KD):
                    last = m.transpose(PSW(2 * (s % 2), KD)[:, k, :], PHR[:, s, 128 * k:128 * k + 128], IDENT)
                last.then_inc(phT_psum, 1)
            pe.wait_ge(par_in, 48)
            for q in range(2):
                for k in range(KD):
                    last = m.transpose(ps[:, 4 + q, NEXP * k:NEXP * k + NEXP], LDP[q][:, 128 * k:128 * k + 128], IDENT[0:NEXP, 0:NEXP])
            last.then_inc(par_psum, 1)
            pe.wait_ge(phT_stored, ST)
            for k in range(KH):
                last = m.transpose(ps[:, k // 8, NEXP * (k % 8):NEXP * (k % 8) + NEXP], pairs(LDB, k), IDENT[0:NEXP, 0:NEXP])
            last.then_inc(par_psum, 1)
            pe.wait_ge(par_stored, 1)
            pe.wait_ge(phn_ready, KD)
            pe.sem_inc(xcT_psum, 2)
            pe.sem_inc(lT_psum, 2)
            pe.sem_inc(cT_psum, 2)
            with pe.Fori(0, NT // 2) as t:
                for s in range(2):
                    pe.wait_ge(xc_ready, t * 2 + (s + 1))
                    pe.wait_ge(xcT_ready, t * 2 + (s + 1))
                    for k in range(KD):
                        last = m.transpose(ps[:, k // 3, NP * (k % 3):NP * (k % 3) + NP], XC[s][:, 128 * k:128 * k + 128], IDENT[0:NP, 0:NP])
                    last.then_inc(xcT_psum, 1)
                for s in range(2):
                    pe.wait_ge(xcT_ready, t * 2 + (s + 2))
                    pe.wait_ge(lc_ready, t * 2 + (s + 1))
                    for f in range(2):
                        for k in range(KD):
                            last = m.matmul(ps[0:NP, 2 + 2 * s + f, :], XCT[s][:, k, :], PHT[:, k, 512 * f:512 * f + 512], start=(k == 0), stop=(k == KD - 1))
                    last.then_inc(l_psum, 1)
                for s in range(2):
                    pe.wait_ge(lc_ready, t * 2 + (s + 3))
                    pe.wait_ge(cT_stored, t * 2 + (s + 1))
                    for k in range(ST):
                        last = m.transpose(PSW(6, ST, NP)[:, k, :], LC[s][:, 128 * k:128 * k + 128], IDENT[0:NP, 0:NP])
                    last.then_inc(lT_psum, 1)
                    pe.wait_ge(cm_taken, t * 2 + (s + 1))
                    pe.wait_ge(cc_ready, t * 2 + (s + 1))
                    for k in range(ST):
                        last = m.transpose(PSW(6, ST, NP)[:, k, :], CC[s][:, 128 * k:128 * k + 128], IDENT[0:NP, 0:NP])
                    last.then_inc(cT_psum, 1)
            pe.wait_ge(diag_ready, 1)
            pe.wait_ge(ones_ready, 2)
            pe.wait_ge(cT_stored, NT + 1)
            for f in range(2):
                last = m.matmul(ps[0:NP, 4 + f, :], ONES[:, 0:NP], DIAG.rearrange("p a b -> p (a b)")[:, 512 * f:512 * f + 512], start=True, stop=True)
            last.then_inc(cmb_psum, 1)
            pe.wait_ge(cmb_stored, 1)
            pe.wait_ge(xh2_stored, NT + 2)
            pe.sem_inc(xs_psum, 2)
            pe.sem_inc(xsT_psum, 1)

            def sums(s, p):
                pe.wait_ge(dexp_ready, s + 1)
                pe.wait_ge(xs_ready, s + 1)
                for f in range(2):
                    for k in range(NT):
                        last = m.matmul(ps[:, 2 * p + f, 0:HALF + f], DC[p][:, k, :], XH2[:, k, f * HALF:f * HALF + HALF + f],
                                        start=(k == 0), stop=(k == NT - 1))
                last.then_inc(xs_psum, 1)

            def flip(s, p):
                pe.wait_ge(xs_ready, s + 3)
                pe.wait_ge(xg_ready, s + 1)
                for k in range(KD):
                    last = m.transpose(PSW(4 + 2 * p, KD)[:, k, :], XSW[:, 128 * k:128 * k + 128], IDENT)
                last.then_inc(xsT_psum, 1)

            def body(s, more):
                sums(s + 1, 1)
                flip(s, 0)
                if more:
                    sums(s + 2, 0)
                flip(s + 1, 1)

            pe.sem_inc(xs_ready, 2)
            pe.sem_inc(xg_ready, 1)
            sums(0, 0)
            with pe.Fori(0, ST // 2 - 1) as t:
                body(t * 2, True)
            body(ST - 2, False)
            pe.wait_ge(xg_ready, ST + 1)
            pe.wait_ge(xgs_zero, 2)
            for free in (hT_psum, part_psum):
                pe.sem_inc(free, 1)
            pe.sem_inc(w_used, RING)

            def up(g, phase):
                pe.wait_ge(xgs_ready, g * SUB + SUB)
                pe.wait_ge(hs_ready, g + 1)
                for u in range(USES):
                    k, b, slot = u // SUB, u % SUB, u % RING
                    pe.wait_ge(w_in[slot], phase * (32 * USES // RING) + 32 * (u // RING + 1))
                    for j in range(HID // 512):
                        for q in range(QUAD):
                            last = m.matmul(ps[32 * q:32 * q + 32, j, :], XGS[:, k, q, PSLOT * b:PSLOT * b + 32],
                                            RG[slot][:, q, 512 * j:512 * j + 512], start=(u == 0), stop=(u == USES - 1), skip_group_check=True)
                    last.then_inc(w_used, 1)

            def turn_h(g):
                pe.wait_ge(hs_ready, g + 2)
                pe.wait_ge(hb_ready, g + 1)
                for k in range(KH):
                    last = m.transpose(ps[:, 5 + k // 4, 128 * (k % 4):128 * (k % 4) + 128], pairs(HS, k), IDENT)
                last.then_inc(hT_psum, 1)

            def down(g, phase):
                pe.wait_ge(h_ready, g + 2)
                pe.wait_ge(ys_ready, g + 1)
                for u in range(USES):
                    k, b, slot = u // SUB, u % SUB, u % RING
                    pe.wait_ge(w_in[slot], phase * (32 * USES // RING) + 32 * (u // RING + 1))
                    for j in range(2):
                        for f in range(2):
                            for q in range(QUAD):
                                last = m.matmul(ps[32 * q:32 * q + 32, 3 + f, 0:HALF], HTS[:, 2 * k + j, q, PSLOT * b:PSLOT * b + 32],
                                                RG[slot][:, q, D * j + HALF * f:D * j + HALF * f + HALF],
                                                start=(u == 0 and j == 0), stop=(u == USES - 1 and j == 1), skip_group_check=True)
                    last.then_inc(w_used, 1)

            def combine(g):
                pe.wait_ge(ys_ready, g + 2)
                pe.wait_ge(ctc_ready, g + 1)
                for n in range(2 * NT):
                    i, f = n // 2, n % 2
                    pe.wait_ge(part_added, g * (2 * NT) + (n + 1))
                    m.matmul(ps[0:NP, 5 + n % NPB, 0:HALF], CTC[:, NP * i:NP * i + NP], YS[:, f * HALF:f * HALF + HALF],
                             start=True, stop=True).then_inc(part_psum, 1)

            with pe.Fori(0, 2) as t:
                up(t, t)
                turn_h(t)
            with pe.Fori(0, 1) as t:
                down(t, t + 2)
            with pe.Fori(0, ST - 2) as t:
                up(t + 2, t * 2 + 3)
                combine(t)
                pe.wait_ge(part_added, t * (2 * NT) + (2 * NT + NPB))
                turn_h(t + 2)
                down(t + 1, t * 2 + 4)
            with pe.Fori(ST - 2, ST - 1) as t:
                combine(t)
                down(t + 1, t * 2 + 3)
                combine(t + 1)



_INS = ["x", "src", "dst", "L0_gnn_W1", "L0_gnn_a_src1", "L0_gnn_a_dst1", "L0_gnn_b1", "L0_gnn_W2", "L0_gnn_a_src2",
        "L0_gnn_a_dst2", "L0_gnn_b2", "L0_ffn_phi", "L0_ffn_ln_g", "L0_ffn_ln_b", "L0_ffn_w1", "L0_ffn_b1",
        "L0_ffn_w2", "L0_ffn_b2"]
_OUTS = [((NODES, D), "float32")]


def kernel(**inputs):
    import numpy as _np
    import concourse.bacc as _bacc
    from concourse import mybir as _mybir
    from concourse.bass_utils import run_bass_kernel_spmd as _run

    nc = _bacc.Bacc("TRN2", target_bir_lowering=False, num_devices=1)
    arrays, args = {}, []
    for name in _INS:
        a = _np.ascontiguousarray(inputs[name])
        arrays[f"in_{name}_dram"] = a
        args.append(nc.dram_tensor(f"in_{name}_dram", a.shape, _mybir.dt.from_np(a.dtype), kind="ExternalInput").ap())
    for i, (shape, dtype) in enumerate(_OUTS):
        dt = _mybir.dt.from_np(_np.dtype(dtype))
        args.append(nc.dram_tensor(f"out_{i}_dram", shape, dt, kind="ExternalOutput").ap())
    gnn_ffn(nc, *args)
    r = _run(nc, [arrays], core_ids=[0])
    return r.results[0]["out_0_dram"]
```

```python
from contextlib import ExitStack

import concourse.bass as bass
from concourse import mybir
from concourse.alu_op_type import AluOpType as ALU

F32 = mybir.dt.float32
BF16 = mybir.dt.bfloat16
F16 = mybir.dt.float16
U16 = mybir.dt.uint16
I32 = mybir.dt.int32
ACT = mybir.ActivationFunctionType
AX_X = mybir.AxisListType.X
RMAX = bass.bass_isa.ReduceOp.max

NODES = 1250
NP = 125
NT = NODES // NP
D = 768
KD = D // 128
HALF = D // 2
HEADS = 8
HC = D // HEADS
EDGES = 40000
NGROUP = 40
ECH = EDGES // NGROUP // NP
PER_PAIR = NGROUP // (NT // 2)
WIN = 50
NWIN = NODES // WIN
SLOPE = 0.2
NO_EDGE = -1e30
MAX_FLOOR = -1e20
EPS_LN = 1e-5
EPS_PHI = 1e-6
EPS_Z = 1e-16
NEXP = 64
PSLOT = 16
SLOTS = NEXP * PSLOT
ST = SLOTS // 128
GE = NEXP // ST
HID = 2 * D
KH = HID // 128
QUAD = 4
SUB = GE // QUAD
RING = 3
RW = QUAD * HID
USES = KD * SUB
PADDED = 3 * PSLOT
NPB = 3


class Chain:

    def __init__(self, eng, sem):
        self.eng, self.sem, self.n, self.base, self.turn = eng, sem, 0, 0, 0

    def step(self, ins):
        ins.then_inc(self.sem, 1)
        self.n += 1
        self.eng.wait_ge(self.sem, self.turn + self.base + self.n)

    def enter(self, i, per):
        self.start, self.per, self.turn = self.n, per, i * per

    def leave(self, count):
        assert self.n - self.start == self.per, (self.n - self.start, self.per)
        self.n, self.turn = self.start, 0
        if isinstance(count, int):
            self.n += count * self.per
        else:
            self.base = count * self.per


def gnn_ffn(nc, x, src, dst, W1, a_src1, a_dst1, b1, W2, a_src2, a_dst2, b2,
            phi, ln_g, ln_b, w1, fb1, w2, fb2, out):
    with ExitStack() as ctx:
        WORDS = 53200
        arena = ctx.enter_context(nc.sbuf_tensor("arena", [128, WORDS], F32))
        ps = ctx.enter_context(nc.psum_tensor("ps", [128, 8, 512], F32))

        def sem(name):
            return ctx.enter_context(nc.semaphore(name))

        def at(off, *shape, parts=128, dtype=F32):
            n = 1
            for s in shape:
                n *= s
            size = 2 if dtype in (BF16, F16, U16) else 4
            words = (n * size + 3) // 4
            assert off + words <= WORDS, (off, words)
            v = arena[0:parts, off:off + words]
            if dtype != F32:
                v = v.bitcast(dtype)
            v = v[:, 0:n]
            if len(shape) == 2:
                v = v.rearrange("p (a b) -> p a b", b=shape[1])
            elif len(shape) == 3:
                v = v.rearrange("p (a b c) -> p a b c", b=shape[1], c=shape[2])
            elif len(shape) == 4:
                v = v.rearrange("p (a b c d) -> p a b c d", b=shape[1], c=shape[2], d=shape[3])
            return v

        H1 = at(0, NT, HEADS, HC + 1, parts=NP)
        CNT_OFF = 7760
        CNT3 = at(CNT_OFF, NT, NODES + WIN, parts=NP, dtype=U16)
        ALS_OFF = CNT_OFF + 6500
        ALS = at(ALS_OFF, HEADS, NODES, parts=NP)
        ALS2 = at(ALS_OFF + 6200, NODES, parts=NP)
        E_OFF = ALS_OFF + 10000
        X = at(E_OFF, NT, D, parts=NP)
        H2 = at(E_OFF, NT, D + 1, parts=NP)
        F_OFF = E_OFF + 7690
        NEGC = at(F_OFF, NODES, parts=NP, dtype=BF16)
        NEGS = at(F_OFF + 625, NT, NODES, parts=NP, dtype=BF16)
        neg_dram = nc.dram_tensor("neg_dram", (NT, NP, NODES), BF16, kind="Internal").ap()
        G_OFF = F_OFF + 6875
        W1A = at(G_OFF, KD, 2, HALF + 8)
        W2A = at(G_OFF, KD, 2, HALF + 1)
        WK = G_OFF + 4704
        TR = [at(WK + 1250 * r, NODES, parts=NP) for r in range(4)]
        TS = [at(F_OFF + 1875 + 1250 * r, NODES, parts=NP) for r in range(2)]
        PR = [at(WK + 5000, NT, NP, parts=NP), at(F_OFF + 4375, NT, NP, parts=NP)]
        O1 = at(WK + 6250, D, parts=NP)
        O1T = at(WK + 7018, KD, NP)
        B1R = at(WK + 7768, D, parts=NP)
        SM = WK + 8536
        IDENT = at(SM, 128)
        ALD = at(SM + 128, NT, HEADS, parts=NP)
        ALD2 = at(SM + 208, NT, parts=NP)
        M0 = at(SM + 218, HEADS, parts=NP)
        TN = at(SM + 226, HEADS, parts=NP)
        NM = at(SM + 234, HEADS, parts=NP)
        NL = at(SM + 320, HEADS, parts=NP)
        ALU8 = at(SM + 328, NT, HEADS, parts=NP)
        ALU8B = at(SM + 408, NT, parts=NP)
        RZ = at(SM + 242, HEADS, parts=NP)
        ALSN = [at(SM + 250 + 8 * s, HEADS, parts=NP) for s in range(2)]
        MV = at(SM + 266, NT, 2, parts=NP)
        MV1 = at(SM + 418, 2, parts=NP)
        BS2 = at(SM + 420, 2, 6, parts=NP)
        ALS2N = at(SM + 306, NT, parts=NP)
        STD = at(SM + 286, NT, parts=NP)
        RSTD = at(SM + 296, NT, parts=NP)
        XH = [at(WK + 768 * s, D, parts=NP) for s in range(2)]
        XT = [at(WK + 1536 + 750 * s, KD, NP) for s in range(2)]
        AVEC = [at(WK + 3036 + 768 * s, 2, HALF) for s in range(2)]
        BST = at(WK + 4600, NT, 2, 6, parts=NP)
        SRCI = at(F_OFF, NGROUP, ECH, parts=NP, dtype=I32)
        DSTI = at(F_OFF + 320, NGROUP, ECH, parts=NP, dtype=I32)
        SRCF = at(F_OFF + 640, NGROUP * ECH, parts=NP)
        DSTF = at(F_OFF + 960, NGROUP, ECH, parts=NP)
        TA = at(F_OFF + 1280, NGROUP * ECH, parts=NP)
        KEYB = at(F_OFF + 1600, NGROUP * ECH, parts=NP)
        KEYA = at(F_OFF + 1920, NGROUP, ECH, parts=NP)
        KEY = at(F_OFF + 2240, NGROUP, ECH, parts=NP)
        TD = at(F_OFF + 2560, NGROUP, ECH, parts=NP)
        MK = at(F_OFF + 2880, NGROUP, ECH, parts=NP)
        GST = at(F_OFF + 3200, 2, NGROUP, parts=NP)
        GAR = at(F_OFF + 3280, 2, NGROUP, parts=NP)
        SPAN = at(F_OFF + 3360, NGROUP, parts=NP)
        FLG = at(F_OFF + 3400, 2, parts=NP)
        D0 = at(F_OFF + 3404, NGROUP, parts=NP)
        D0I = at(F_OFF + 3444, NGROUP, parts=NP, dtype=I32)
        WPI = at(F_OFF + 3484, 1, parts=NP, dtype=I32)
        IOI = at(F_OFF + 3500, NT * WIN, parts=NP, dtype=I32)
        IOB = at(F_OFF + 4000, 128, parts=NP, dtype=F16)
        IOK = at(F_OFF + 4064, NT * WIN, parts=NP, dtype=F16)
        OHR = ECH
        KEYBH = at(F_OFF + 4320, NGROUP, ECH, parts=NP, dtype=F16)
        OB = [at(WK + 5000 + 512 * s, ECH, 128, parts=NP, dtype=F16) for s in range(2)]
        OK = [at(F_OFF + 4576 + 250 * r, NT * WIN, parts=NP, dtype=F16) for r in range(OHR)]
        CF = [at(WK + 1250 * r, NT, NP, parts=NP) for r in range(2)]
        AW = [at(768 * r, 2, HALF) for r in range(2)]
        AW2 = [at(E_OFF + D * r, 2, HALF) for r in range(10)] + [at(WK + 6250, 2, HALF)]
        EL = at(F_OFF + 625, D, parts=NP)
        PHR = at(ALS_OFF, ST, D)
        B2R = at(WK + 7768, D, parts=NP)

        X2 = at(0, NT, D, parts=NP)
        CT_OFF = 7760
        CT = at(CT_OFF, ST, NODES)
        XH2_OFF = CT_OFF + 10000
        XH2 = at(XH2_OFF, NT, D + 1, parts=NP)
        L_OFF = XH2_OFF + 7690
        L = at(L_OFF, NT, SLOTS, parts=NP)
        PHT_OFF = XH2_OFF + RING * RW
        assert PHT_OFF >= L_OFF + NT * SLOTS
        PHT = at(PHT_OFF, KD, SLOTS)
        XGT = at(PHT_OFF, KD, SLOTS)
        CM_OFF = PHT_OFF + 6144
        CMB = at(CM_OFF, SLOTS, parts=NP)
        PRE_OFF = CM_OFF + 1024
        GT = at(PRE_OFF, KD, NEXP)
        BT = at(PRE_OFF + 1152, KD, NEXP)
        FB1T = at(PRE_OFF + 384, KH, NEXP)
        FW = PRE_OFF + 1536
        XC = [at(FW + 768 * s, D, parts=NP) for s in range(2)]
        XCT = [at(FW + 1536 + 750 * s, KD, NP) for s in range(2)]
        XSW = at(FW, D)
        LC = [at(FW + 3040, SLOTS, parts=NP), at(FW + 5988, SLOTS, parts=NP)]
        CC = [at(FW + 4064, SLOTS, parts=NP), at(CM_OFF, SLOTS, parts=NP)]
        DIAG = at(FW + 3040, ST, 128)
        DC = [at(FW + 1536, NT, 128, parts=NP), at(FW + 2816, NT, 128, parts=NP)]
        SM2 = FW + 5088
        assert SM2 + 900 + SLOTS <= SM, (SM2, SM)
        CMX = at(SM2, ST, NT)
        CMN = at(SM2 + 80, ST)
        ONES = at(SM2 + 230, 128)
        NRM = at(SM2 + 360, KD, PSLOT)
        NRR = at(SM2 + 456, KD, PSLOT)
        RM = [at(SM2 + 580 + s, 1, parts=NP) for s in range(2)]
        RS = [at(SM2 + 582 + s, 1, parts=NP) for s in range(2)]
        RI = [at(SM2 + 584 + s, 1, parts=NP) for s in range(2)]
        CSI = at(SM2 + 555, 1)
        SST = at(SM2 + 556, 2, 6)
        SMV = at(SM2 + 568, 2)
        SSD = at(SM2 + 570, 1)
        SRD = at(SM2 + 571, 1)
        SQ = [at(FW + KD * 128 * s, KD, 128) for s in range(2)]
        NRP = at(FW + 3584, ST, KD, PSLOT)
        LDP = [at(FW + 2048, D, parts=NEXP), at(FW + 2816, D, parts=NEXP)]
        LDB = at(L_OFF, HID, parts=NEXP)
        RG = [at(XH2_OFF + RW * (RING - 1 - s), QUAD, HID) for s in range(RING)]
        assert XH2_OFF + RW * (RING - 1) >= L_OFF
        CTC = at(CM_OFF, NODES)
        XGS = at(FW - 128, KD, QUAD, PADDED)
        HTS = at(FW + 1024, KH, QUAD, PADDED)
        HS = at(FW + 3328, HID)
        HB = at(FW + 4864, KH, 128)
        YS = at(SM + 128, D)
        B2G = at(FW + 6400, D)
        assert CM_OFF + NODES <= PRE_OFF + 384 and FW + 7168 <= SM

        L1_STEPS = 2 * HEADS + 6

        def PST(k, n, bank):
            v = ps[:, bank:min(bank + 3, 8), :].rearrange("p a (b n) -> p (a b) n", n=128)
            return v[:, k:k + n, 0:NP]

        def PSW(bank, n, width=128):
            return ps[:, bank:bank + 2, :].rearrange("p a (b n) -> p (a b) n", n=128)[:, 0:n, 0:width]

        def pairs(v, k):
            return v.rearrange("p (c n j) -> p c j n", j=2, n=128)[:, k // 2, k % 2, :]

        def w1_done(g):
            return RING + USES if isinstance(g, int) and g == 0 else g * (2 * USES) + RING

        def w2_done(g):
            return RING + 2 * ST * USES if isinstance(g, int) and g == ST - 1 else g * (2 * USES) + (RING + 3 * USES)

        x_in = sem("x_in"); w1_in = sem("w1_in"); avec_in = sem("avec_in"); edges_in = sem("edges_in")
        b1row_in = sem("b1row_in"); w2_in = sem("w2_in"); avec2_in = sem("avec2_in"); x_again = sem("x_again")
        b2row_in = sem("b2row_in"); phi_in = sem("phi_in"); par_in = sem("par_in"); 
        ident_ready = sem("ident_ready"); iota_ready = sem("iota_ready"); cnt_zero = sem("cnt_zero")
        dve_c = sem("dve_c"); count_c = sem("count_c"); attend_c = sem("attend_c"); act_c = sem("act_c"); pool_c = sem("pool_c")
        span_ready = sem("span_ready"); span_all = sem("span_all"); windows_ready = sem("windows_ready")
        aw_ready = sem("aw_ready"); aw2_ready = sem("aw2_ready"); wa_ready = sem("wa_ready"); h1_ones = sem("h1_ones")
        var_ready = sem("var_ready"); std_ready = sem("std_ready")
        xhat_ready = sem("xhat_ready"); xT_psum = sem("xT_psum"); xT_ready = sem("xT_ready")
        h1_psum = sem("h1_psum"); h1_stored = sem("h1_stored"); als_psum = sem("als_psum"); als_stored = sem("als_stored")
        onehot_ready = sem("onehot_ready"); chunk_counted = sem("chunk_counted"); group_added = sem("group_added"); cnt_done = sem("cnt_done"); keys_known = sem("keys_known"); slot_taken = sem("slot_taken")
        cnt_tile = sem("cnt_tile"); cntT_psum = sem("cntT_psum"); neg_ready = sem("neg_ready")
        neg_in = sem("neg_in"); neg_saved = sem("neg_saved"); upper_ready = sem("upper_ready"); summed = sem("summed"); ald_scaled = sem("ald_scaled"); masked = sem("masked"); shift_ready = sem("shift_ready")
        e_ready = sem("e_ready"); eT_psum = sem("eT_psum"); p_ready = sem("p_ready"); o_psum = sem("o_psum")
        elu_in = sem("elu_in"); elu_exp = sem("elu_exp"); o1_ready = sem("o1_ready")
        o_free = sem("o_free"); o1T_psum = sem("o1T_psum"); o1T_ready = sem("o1T_ready"); h2_psum = sem("h2_psum"); h2_stored = sem("h2_stored")
        als2_psum = sem("als2_psum"); als2_stored = sem("als2_stored"); wa2_ready = sem("wa2_ready"); h2_ones = sem("h2_ones")
        neg2_in = sem("neg2_in"); upper2_ready = sem("upper2_ready"); summed2 = sem("summed2"); ald2_scaled = sem("ald2_scaled"); masked2 = sem("masked2"); shift2_ready = sem("shift2_ready")
        e2_ready = sem("e2_ready"); eT2_psum = sem("eT2_psum"); p2_ready = sem("p2_ready"); o2_psum = sem("o2_psum")
        x2_ready = sem("x2_ready"); xb_ready = sem("xb_ready")
        phT_psum = sem("phT_psum"); phT_stored = sem("phT_stored"); nrm_ready = sem("nrm_ready"); ones_ready = sem("ones_ready")
        second_c = sem("second_c"); expert_c = sem("expert_c"); logit_c = sem("logit_c"); input_c = sem("input_c"); nrs_ready = sem("nrs_ready")
        sq_ready = sem("sq_ready"); sq_used = sem("sq_used"); phn_ready = sem("phn_ready"); par_psum = sem("par_psum"); par_stored = sem("par_stored")
        var2_ready = sem("var2_ready"); std2_ready = sem("std2_ready")
        xc_ready = sem("xc_ready"); xh2_stored = sem("xh2_stored"); xcT_psum = sem("xcT_psum"); xcT_ready = sem("xcT_ready")
        l_psum = sem("l_psum"); lc_ready = sem("lc_ready"); l_stored = sem("l_stored"); rm_ready = sem("rm_ready")
        ce_ready = sem("ce_ready"); cc_ready = sem("cc_ready"); lT_psum = sem("lT_psum"); cm_taken = sem("cm_taken")
        cT_psum = sem("cT_psum"); cT_stored = sem("cT_stored")
        diag_ready = sem("diag_ready"); cmb_psum = sem("cmb_psum"); cmb_stored = sem("cmb_stored")
        ds_ready = sem("ds_ready"); dexp_ready = sem("dexp_ready"); xs_psum = sem("xs_psum"); xsv_ready = sem("xsv_ready")
        xstd_ready = sem("xstd_ready"); xs_ready = sem("xs_ready"); xsT_psum = sem("xsT_psum"); xg_ready = sem("xg_ready")
        w_in = [sem(f"w_in{s}") for s in range(RING)]
        w_used = sem("w_used"); xgs_zero = sem("xgs_zero"); xgs_ready = sem("xgs_ready"); hs_ready = sem("hs_ready")
        hT_psum = sem("hT_psum"); hb_ready = sem("hb_ready"); h_ready = sem("h_ready"); ys_ready = sem("ys_ready")
        b2g_in = sem("b2g_in"); ctc_ready = sem("ctc_ready")
        part_psum = sem("part_psum"); part_added = sem("part_added"); out_done = sem("out_done")


        block = ctx.enter_context(nc.Block())

        @block.sync
        def _(sp):
            for v, a in ((SRCI, src), (DSTI, dst)):
                sp.dma_start(v, a.rearrange("(g p j) -> p g j", p=NP, j=ECH)).then_inc(edges_in, 16)
            for v, a in zip(AVEC, (a_src1, a_dst1)):
                sp.dma_start(v.rearrange("p f c -> p (f c)"), a.rearrange("h c -> (h c)")[None, :].to_broadcast([128, D])).then_inc(avec_in, 16)
            for k in range(KD):
                sp.dma_start(W1A[:, k, :, 0:HALF], W1[128 * k:128 * k + 128, :].rearrange("p (f c) -> p f c", f=2)).then_inc(w1_in, 16)
            for i in range(NT):
                sp.dma_start(X[:, i, :], x[NP * i:NP * i + NP, :]).then_inc(x_in, 16)
            sp.dma_start(B1R, b1[None, :].to_broadcast([NP, D])).then_inc(b1row_in, 16)
            sp.wait_ge(h1_psum, NT)
            for k in range(KD):
                sp.dma_start(W2A[:, k, :, 0:HALF], W2[128 * k:128 * k + 128, :].rearrange("p (f c) -> p f c", f=2)).then_inc(w2_in, 16)
            for v, a in zip(AVEC, (a_src2, a_dst2)):
                sp.dma_start(v.rearrange("p f c -> p (f c)"), a[0:1, :].to_broadcast([128, D])).then_inc(avec2_in, 16)
            with sp.Fori(0, NT // 2) as t:
                for s in range(2):
                    sp.wait_ge(neg_ready, t * 2 + (s + 1) + 1)
                    sp.dma_start(neg_dram[bass.ds(t * 2 + s, 1)].rearrange("o p n -> p (o n)"), NEGS[:, bass.ds(t * 2 + s, 1), :].rearrange("p o n -> p (o n)")).then_inc(neg_saved, 16)
            sp.wait_ge(neg_saved, 16 * NT)
            with sp.Fori(0, NT) as i:
                sp.wait_ge(masked, i * HEADS + 1)
                sp.dma_start(NEGC, neg_dram[bass.ds(i, 1)].rearrange("o p n -> p (o n)")).then_inc(neg_in, 16)
            sp.wait_ge(masked, NT * HEADS + 1)
            sp.dma_start(NEGC, neg_dram[0]).then_inc(neg2_in, 16)
            sp.wait_ge(o_psum, NT * HEADS + 2)
            for i in range(NT):
                sp.dma_start(X2[:, i, :], x[NP * i:NP * i + NP, :]).then_inc(x_again, 16)
            sp.dma_start(PHR, phi.rearrange("n p d -> (n p) d").rearrange("(t q) d -> q t d", q=128)).then_inc(phi_in, 16)
            sp.wait_ge(o1_ready, NT + 1)
            sp.dma_start(B2R, b2[None, :].to_broadcast([NP, D])).then_inc(b2row_in, 16)
            with sp.Fori(1, NT) as i:
                sp.wait_ge(masked2, i)
                sp.dma_start(NEGC, neg_dram[bass.ds(i, 1)].rearrange("o p n -> p (o n)")).then_inc(neg2_in, 16)
            sp.wait_ge(x2_ready, NT + 2)
            for v, a in zip(LDP, (ln_g, ln_b)):
                sp.dma_start(v, a).then_inc(par_in, 16)
            sp.dma_start(LDB, fb1).then_inc(par_in, 16)

            def fetch(weights, g, phase):
                for u in range(USES):
                    k, b, slot = u // SUB, u % SUB, u % RING
                    if isinstance(phase, int) and u == 0:
                        sp.wait_ge(ds_ready, ST)
                    elif isinstance(phase, int) and u < RING:
                        sp.wait_ge(xs_psum, ST + 2)
                    else:
                        sp.wait_ge(w_used, phase * USES + (u + 1))
                    for q in range(0, QUAD, 2):
                        e = g * GE + (SUB * q + b)
                        if weights is w1:
                            rows = w1[bass.ds(e, 2, step=SUB), 128 * k:128 * k + 128, :].rearrange("q p h -> p q h")
                        else:
                            rows = w2[bass.ds(e, 2, step=SUB), 256 * k:256 * k + 256, :].rearrange("q (p j) d -> p q (j d)", j=2)
                        sp.dma_start(RG[slot][:, q:q + 2, :], rows).then_inc(w_in[slot], 16)

            def fetch_b2(g):
                sp.wait_ge(ys_ready, g + 1)
                for e in range(GE):
                    sp.dma_start(B2G[PSLOT * e:PSLOT * e + PSLOT, :], fb2[bass.ds(g * GE + e, 1), :].to_broadcast([PSLOT, D])).then_inc(b2g_in, 16)

            fetch(w1, 0, 0)
            with sp.Fori(0, ST - 1) as t:
                fetch(w1, t + 1, t * 2 + 1)
                fetch_b2(t)
                fetch(w2, t, t * 2 + 2)
            with sp.Fori(ST - 1, ST) as t:
                fetch_b2(t)
                fetch(w2, t, t * 2 + 1)
            for i in range(NT):
                sp.wait_ge(part_added, 2 * NT * (ST - 1) + 2 * i + 2 + NPB)
                sp.dma_start(out[NP * i:NP * i + NP, :], X2[:, i, :]).then_inc(out_done, 16)
            sp.wait_ge(out_done, 16 * NT)


        @block.gpsimd
        def _(pool):
            g = nc.gpsimd
            c = Chain(pool, pool_c)
            c.step(g.memset(IDENT, 0.0))
            g.affine_select(out=IDENT, in_=IDENT, compare_op=ALU.not_equal, fill=1.0, base=0,
                            pattern=[[-1, 128]], channel_multiplier=1).then_inc(ident_ready, 1)
            g.iota(IOI, pattern=[[1, NT * WIN]], base=1, channel_multiplier=0).then_inc(iota_ready, 1)
            g.memset(at(CNT_OFF, NT * (NODES + WIN) // 2, parts=NP), 0.0).then_inc(cnt_zero, 1)
            pool.wait_ge(span_ready, 2)
            g.partition_all_reduce(GAR.rearrange("p a b -> p (a b)"), GST.rearrange("p a b -> p (a b)"), NP, RMAX).then_inc(span_all, 1)
            pool.wait_ge(avec_in, 32)
            pool.wait_ge(w1_in, 16 * KD)
            for k in range(KD):
                for q in range(2):
                    if k:
                        pool.wait_ge(wa_ready, 2 * k + q - 1)
                    g.tensor_tensor(AW[q], W1A[:, k, :, 0:HALF], AVEC[q], ALU.mult).then_inc(aw_ready, 1)
            pool.wait_ge(wa_ready, 2 * KD)
            g.memset(H1[:, :, :, HC:HC + 1], 1.0).then_inc(h1_ones, 1)
            pool.wait_ge(xhat_ready, NT)
            pool.wait_ge(w2_in, 16 * KD)
            pool.wait_ge(avec2_in, 32)
            for k in range(KD):
                for q in range(2):
                    n = 2 * k + q
                    if n >= len(AW2):
                        pool.wait_ge(wa2_ready, n - len(AW2) + 1)
                    g.tensor_tensor(AW2[n % len(AW2)], W2A[:, k, :, 0:HALF], AVEC[q], ALU.mult).then_inc(aw2_ready, 1)
            pool.sem_inc(summed, 2)
            with pool.Fori(0, NT) as i:
                for h in range(HEADS):
                    pool.wait_ge(upper_ready, i * HEADS + (h + 1))
                    g.tensor_tensor(TR[h % 4], TR[h % 4], TS[h % 2], ALU.add).then_inc(summed, 1)
            pool.wait_ge(h2_stored, NT + 1)
            g.memset(H2[:, :, D:D + 1], 1.0).then_inc(h2_ones, 1)
            pool.sem_inc(summed2, 2)

            def leaky2(i, s):
                pool.wait_ge(upper2_ready, i + 1)
                g.tensor_tensor(TR[s], TR[s], TS[s], ALU.add).then_inc(summed2, 1)

            for s in range(2):
                leaky2(s, s)
            pool.wait_ge(x_again, 16 * NT)
            pool.wait_ge(b2row_in, 16)
            for i in range(NT):
                g.tensor_tensor(X2[:, i, :], X2[:, i, :], B2R, ALU.add).then_inc(xb_ready, 1)
                if i == 1 or i == 3:
                    for s in range(2):
                        leaky2(i + 1 + s, s)
            with pool.Fori(3, NT // 2) as t:
                for s in range(2):
                    leaky2(t * 2 + s, s)
            pool.wait_ge(phT_psum, ST)
            pool.wait_ge(x2_ready, NT + 2)
            g.memset(ONES, 1.0).then_inc(ones_ready, 1)
            g.memset(XH2[:, :, D:D + 1], 1.0).then_inc(ones_ready, 1)
            pool.sem_inc(xh2_stored, 2)
            pool.sem_inc(l_stored, 2)

            def keep_x(i, s):
                pool.wait_ge(xc_ready, i + 1)
                g.tensor_copy(XH2[:, bass.ds(i, 1), 0:D].rearrange("p o d -> p (o d)"), XC[s]).then_inc(xh2_stored, 1)

            def keep_l(i, s):
                pool.wait_ge(lc_ready, i + 3)
                g.tensor_copy(L[:, bass.ds(i, 1), :].rearrange("p o d -> p (o d)"), LC[s]).then_inc(l_stored, 1)

            for s in range(2):
                keep_x(s, s)
            with pool.Fori(0, NT // 2 - 1) as t:
                for s in range(2):
                    keep_l(t * 2 + s, s)
                    keep_x(t * 2 + (s + 2), s)
            for s in range(2):
                keep_l(NT - 2 + s, s)
            pool.wait_ge(xg_ready, ST + 1)
            pool.wait_ge(cT_stored, NT + 1)
            for v in (XGS, HTS):
                g.memset(v.rearrange("p k q c -> p (k q) c")[:, :, PSLOT:2 * PSLOT], 0.0).then_inc(xgs_zero, 1)

            def spaced(i):
                for b in range(SUB):
                    g.tensor_copy(XGS[:, :, :, 2 * PSLOT * b:2 * PSLOT * b + PSLOT],
                                  XGT[:, :, bass.ds(i * 128, 128)].rearrange("p k (q b r) -> p k q b r", b=SUB, r=PSLOT)[:, :, :, b, :]).then_inc(xgs_ready, 1)

            def weights(i):
                g.tensor_copy(CTC, CT[:, bass.ds(i, 1), :].rearrange("p o n -> p (o n)")).then_inc(ctc_ready, 1)

            spaced(0)
            weights(0)
            pool.wait_ge(w_used, w1_done(0))
            spaced(1)
            with pool.Fori(2, ST) as i:
                pool.wait_ge(w_used, (i - 1) * (2 * USES) + RING)
                spaced(i)
                pool.wait_ge(part_psum, (i - 1) * (2 * NT) + 1)
                weights(i - 1)
            pool.wait_ge(part_psum, (ST - 1) * (2 * NT) + 1)
            weights(ST - 1)


        @block.scalar
        def _(act):
            a = nc.scalar
            c = Chain(act, act_c)
            for free in (als_stored, h1_stored, h2_stored):
                act.sem_inc(free, 1)
            act.wait_ge(var_ready, 1)
            a.activation(STD, STD, ACT.Sqrt).then_inc(std_ready, 1)

            def x_turned(t, s):
                act.wait_ge(xT_psum, t * 2 + (s + 1) + 1)
                for f in range(2):
                    last = a.copy(XT[s][:, 3 * f:3 * f + 3, :], ps[:, f, 0:375].rearrange("p (a b) -> p a b", b=NP))
                last.then_inc(xT_ready, 1)

            def features_out(t, s):
                act.wait_ge(h1_psum, t * 2 + (s + 1))
                act.wait_ge(h1_ones, 1)
                for f in range(2):
                    a.copy(H1[:, bass.ds(t * 2 + s, 1), 4 * f:4 * f + 4, 0:HC].rearrange("p o h c -> p (o h) c"),
                           ps[0:NP, 4 + 2 * s + f, 0:HALF].rearrange("p (h c) -> p h c", c=HC))
                a.copy(ALD[:, bass.ds(t * 2 + s, 1), :].rearrange("p o h -> p (o h)"), ps[0:NP, 5 + 2 * s, HALF:HALF + 8])
                a.copy(ALSN[s], ps[0:NP, 4 + 2 * s, HALF:HALF + 8]).then_inc(h1_stored, 1)

            def terms_out(t, s):
                act.wait_ge(als_psum, t * 2 + (s + 1))
                a.copy(ALS[:, :, bass.ds((t * 2 + s) * NP, NP)],
                       ps[0:NP, 4 + 2 * s:6 + 2 * s, :].rearrange("p a (b n) -> p (a b) n", n=128)[:, :, 0:NP]).then_inc(als_stored, 1)

            with act.Fori(0, NT // 2) as t:
                x_turned(t, 0)
                features_out(t, 0)
                x_turned(t, 1)
                terms_out(t, 0)
                features_out(t, 1)
                terms_out(t, 1)
            act.wait_ge(cnt_done, 1)
            with act.Fori(0, NT // 2) as t:
                for s in range(2):
                    act.wait_ge(cntT_psum, t * 2 + 1)
                    a.copy(CF[s], CNT3[:, :, bass.ds((t * 2 + s) * NP, NP)]).then_inc(cnt_tile, 1)
            def second_vectors(first, last):
                for n in range(first, last):
                    act.wait_ge(aw2_ready, n + 1)
                    w = AW2[n % len(AW2)]
                    a.activation(w, w, ACT.Identity, accum_out=W2A[:, n // 2, n % 2, HALF:HALF + 1]).then_inc(wa2_ready, 1)

            second_vectors(0, 2)
            act.wait_ge(ald_scaled, 1)
            act.wait_ge(neg_saved, 16 * NT)
            def upper(i, h):
                act.wait_ge(masked, i * HEADS + (h + 1) + 1)
                act.wait_ge(summed, i * HEADS + (h + 1))
                a.activation(TS[h % 2], TR[h % 4], ACT.Relu, scale=(1 - SLOPE) / SLOPE,
                             bias=ALU8[:, bass.ds(i, 1), h:h + 1].rearrange("p a b -> p (a b)")).then_inc(upper_ready, 1)

            def exponential(i, h):
                act.wait_ge(shift_ready, i * HEADS + (h + 1))
                act.wait_ge(summed, i * HEADS + (h + 3))
                a.activation(TR[h % 4], TR[h % 4], ACT.Exp, bias=NL[:, h:h + 1]).then_inc(e_ready, 1)

            def elu_part(i):
                act.wait_ge(elu_in, i + 1)
                a.activation(EL, EL, ACT.Exp).then_inc(elu_exp, 1)

            def by_feature(i):
                act.wait_ge(o1T_psum, i + 1)
                for f in range(2):
                    last = a.copy(O1T[:, 3 * f:3 * f + 3, :], ps[:, f, 0:375].rearrange("p (a b) -> p a b", b=NP))
                last.then_inc(o1T_ready, 1)

            def projected(i):
                act.wait_ge(h2_psum, i + 1)
                for f in range(2):
                    a.copy(H2[:, bass.ds(i, 1), f * HALF:f * HALF + HALF].rearrange("p o d -> p (o d)"), ps[0:NP, 3 + f, 0:HALF])
                a.copy(ALD2[:, bass.ds(i, 1)], ps[0:NP, 4, HALF:HALF + 1])
                a.copy(ALS2N[:, bass.ds(i, 1)], ps[0:NP, 3, HALF:HALF + 1]).then_inc(h2_stored, 1)

            def tile1(i, before, more):
                for h in range(HEADS):
                    if h == 4 and before:
                        elu_part(i - 1)
                    if h == 6 and before:
                        by_feature(i - 1)
                    if h + 1 < HEADS:
                        upper(i, h + 1)
                    elif more:
                        upper(i + 1, 0)
                    exponential(i, h)
                    if not before and 2 <= h < HEADS - 1:
                        second_vectors(2 * h - 2, 2 * h)
                if before:
                    projected(i - 1)

            upper(0, 0)
            tile1(0, False, True)
            with act.Fori(1, NT - 1) as i:
                tile1(i, True, True)
            tile1(NT - 1, True, False)
            elu_part(NT - 1)
            by_feature(NT - 1)
            projected(NT - 1)
            act.wait_ge(als2_psum, 1)
            a.copy(ALS2.rearrange("p (a n) -> p a n", n=NP), PST(0, NT, 0)[0:NP]).then_inc(als2_stored, 1)
            act.wait_ge(ald2_scaled, 1)
            with act.Fori(0, NT // 2) as t:
                for s in range(2):
                    i = t * 2 + s
                    act.wait_ge(masked2, t * 2 + (s + 1))
                    act.wait_ge(summed2, t * 2 + (s + 1))
                    a.activation(TS[s], TR[s], ACT.Relu, scale=(1 - SLOPE) / SLOPE, bias=ALU8B[:, bass.ds(i, 1)]).then_inc(upper2_ready, 1)
                    act.wait_ge(shift2_ready, t * 2 + (s + 1))
                    act.wait_ge(summed2, t * 2 + (s + 3))
                    a.activation(TR[s], TR[s], ACT.Exp, bias=NL[:, s:s + 1]).then_inc(e2_ready, 1)
            act.wait_ge(var2_ready, 1)
            a.activation(STD, STD, ACT.Sqrt).then_inc(std2_ready, 1)
            for s in range(ST):
                act.wait_ge(phT_psum, s + 1)
                if s >= 2:
                    act.wait_ge(sq_used, s - 1)
                a.activation(SQ[s % 2], PSW(2 * (s % 2), KD), ACT.Square).then_inc(sq_ready, 1)
                a.copy(PHT[:, :, 128 * s:128 * s + 128], PSW(2 * (s % 2), KD)).then_inc(phT_stored, 1)
            act.wait_ge(par_psum, 1)
            for q, w in enumerate((GT, BT)):
                a.copy(w, ps[:, 4 + q, 0:KD * NEXP].rearrange("p (k n) -> p k n", n=NEXP))
            act.wait_ge(par_psum, 2)
            a.copy(FB1T[:, 0:8, :], ps[:, 0, :].rearrange("p (k n) -> p k n", n=NEXP))
            a.copy(FB1T[:, 8:12, :], ps[:, 1, 0:4 * NEXP].rearrange("p (k n) -> p k n", n=NEXP)).then_inc(par_stored, 1)
            act.wait_ge(nrm_ready, 1)
            a.activation(NRM, NRM, ACT.Sqrt).then_inc(nrs_ready, 1)
            act.sem_inc(xcT_ready, 1)
            act.sem_inc(lc_ready, 2)
            act.sem_inc(cT_stored, 1)

            def x_by_feature(i, s):
                act.wait_ge(xcT_psum, i + 3)
                for f in range(2):
                    last = a.copy(XCT[s][:, 3 * f:3 * f + 3, :], ps[:, f, 0:375].rearrange("p (a b) -> p a b", b=NP))
                last.then_inc(xcT_ready, 1)

            def logits(i, s):
                act.wait_ge(l_psum, i + 1)
                act.wait_ge(l_stored, i + 1)
                act.wait_ge(lT_psum, i + 1)
                a.copy(LC[s].rearrange("p (a n) -> p a n", n=512), ps[0:NP, 2 + 2 * s:4 + 2 * s, :]).then_inc(lc_ready, 1)

            def combine_exp(i, s):
                act.wait_ge(rm_ready, i + 1)
                act.wait_ge(cT_psum, i + 1)
                a.activation(CC[s], LC[s], ACT.Exp, bias=RM[s], accum_out=RS[s]).then_inc(ce_ready, 1)

            def combine_out(i):
                act.wait_ge(cT_psum, i + 3)
                a.copy(CT[:, :, bass.ds(i * NP, NP)], PSW(6, ST, NP)).then_inc(cT_stored, 1)

            for s in range(2):
                x_by_feature(s, s)
            logits(0, 0)
            combine_exp(0, 0)
            with act.Fori(0, NT // 2 - 1) as t:
                for s in (1, 0):
                    i = t * 2 + (2 - s)
                    x_by_feature(i + 1, 1 - s)
                    logits(i, s)
                    combine_out(i - 1)
                    combine_exp(i, s)
            logits(NT - 1, 1)
            combine_out(NT - 2)
            combine_exp(NT - 1, 1)
            combine_out(NT - 1)
            act.wait_ge(cmb_psum, 1)
            a.copy(CMB.rearrange("p (a n) -> p a n", n=512), ps[0:NP, 4:6, :]).then_inc(cmb_stored, 1)

            def disp(s, p):
                act.wait_ge(ds_ready, s + 1)
                a.activation(DC[p], DC[p], ACT.Exp).then_inc(dexp_ready, 1)

            def spread(s):
                act.wait_ge(xsv_ready, s + 1)
                a.activation(SSD, SSD, ACT.Sqrt).then_inc(xstd_ready, 1)

            def body(t, more):
                for s in range(2):
                    if more:
                        disp(2 * t + (s + 2), s)
                    spread(2 * t + s)

            disp(0, 0)
            disp(1, 1)
            with act.Fori(0, ST // 2 - 1) as t:
                body(t, True)
            body(ST // 2 - 1, False)
            act.wait_ge(xgs_zero, 2)
            act.sem_inc(hs_ready, 1)
            act.sem_inc(h_ready, 1)

            def hidden(g):
                act.wait_ge(w_used, w1_done(g))
                act.wait_ge(hT_psum, g + 1)
                a.copy(HS.rearrange("p (j n) -> p j n", n=512), ps[:, 0:3, :]).then_inc(hs_ready, 1)
                act.wait_ge(hb_ready, g + 2)
                if not isinstance(g, int):
                    act.wait_ge(w_used, g * (2 * USES) + (RING + USES))
                for b in range(SUB):
                    last = a.activation(HTS.rearrange("p k q c -> p (k q) c")[:, :, 2 * PSLOT * b:2 * PSLOT * b + PSLOT],
                                        HB.rearrange("p k (q b r) -> p (k q) b r", b=SUB, r=PSLOT)[:, :, b, :], ACT.Gelu)
                last.then_inc(h_ready, 1)

            hidden(0)
            with act.Fori(1, ST) as g:
                hidden(g)


        @block.vector
        def _(dve):
            v = nc.vector
            c = Chain(dve, dve_c)
            for free in (masked, group_added, o1_ready, neg_ready):
                dve.sem_inc(free, 1)
            dve.sem_inc(group_added, 1)
            dve.wait_ge(edges_in, 32)
            c.step(v.tensor_copy(SRCF, SRCI.rearrange("p g j -> p (g j)")))
            c.step(v.tensor_copy(DSTF, DSTI))
            v.tensor_reduce(GST[:, 1, :], DSTF, AX_X, ALU.max).then_inc(span_ready, 1)
            c.step(v.tensor_reduce(GST[:, 0, :], DSTF, AX_X, ALU.min))
            v.tensor_scalar(GST[:, 0, :], GST[:, 0, :], -1.0, None, ALU.mult).then_inc(span_ready, 1)
            def stats(i):
                for f in range(2):
                    c.step(v.bn_stats(BST[:, i, f, :], X[:, i, f * HALF:f * HALF + HALF]))
                c.step(v.bn_aggr(MV[:, i, :], BST[:, i, :, :].rearrange("p f s -> p (f s)")))

            for n in range(2 * KD):
                dve.wait_ge(aw_ready, n + 1)
                v.tensor_reduce(W1A[:, n // 2, n % 2, HALF:HALF + HEADS], AW[n % 2].rearrange("p f (h c) -> p (f h) c", c=HC),
                                AX_X, ALU.add).then_inc(wa_ready, 1)
                if n == KD:
                    dve.wait_ge(x_in, 16 * NT)
                if n >= KD:
                    for i in range(2 * (n - KD), min(NT, 2 * (n - KD) + 2)):
                        stats(i)
            v.tensor_scalar(STD, MV[:, :, 1], EPS_LN, None, ALU.add).then_inc(var_ready, 1)
            dve.wait_ge(std_ready, 1)
            c.step(v.reciprocal(RSTD, STD))

            def normalise(i, s):
                if not isinstance(i, int):
                    dve.wait_ge(xT_psum, i)
                v.tensor_scalar(XH[s], X[:, bass.ds(i, 1), :].rearrange("p o d -> p (o d)"),
                                MV[:, bass.ds(i, 1), 0:1].rearrange("p a b -> p (a b)"), RSTD[:, bass.ds(i, 1)],
                                ALU.subtract, ALU.mult).then_inc(xhat_ready, 1)

            for s in range(2):
                normalise(s, s)
            c.step(v.tensor_scalar(TA, SRCF, float(NP), None, ALU.is_ge))
            for k in range(2, NT):
                c.step(v.scalar_tensor_tensor(out=TA, in0=SRCF, scalar=float(NP * k), in1=TA, op0=ALU.is_ge, op1=ALU.add))
            c.step(v.scalar_tensor_tensor(out=KEYB, in0=TA, scalar=-float(NP), in1=SRCF, op0=ALU.mult, op1=ALU.add))
            c.step(v.tensor_copy(KEYBH.rearrange("p g j -> p (g j)"), KEYB))
            c.step(v.tensor_scalar(KEYA.rearrange("p g j -> p (g j)"), TA, float(WIN), 1.0, ALU.mult, ALU.add))
            dve.wait_ge(iota_ready, 1)
            c.step(v.tensor_copy(IOK, IOI))
            c.step(v.tensor_scalar(IOB, IOI[:, 0:128], -1.0, None, ALU.add))
            dve.wait_ge(span_all, 1)
            c.step(v.tensor_tensor(SPAN, GAR[:, 0, :], GAR[:, 1, :], ALU.add))
            c.step(v.tensor_reduce(FLG[:, 0:1], SPAN, AX_X, ALU.max))
            c.step(v.tensor_scalar(FLG[:, 1:2], FLG[:, 0:1], WIN - 0.5, None, ALU.is_lt))
            c.step(v.tensor_scalar(WPI, FLG[:, 1:2], 1.0 - NWIN, float(NWIN), ALU.mult, ALU.add))
            v.tensor_scalar(D0, GAR[:, 0, :], -1.0, FLG[:, 1:2], ALU.mult, ALU.mult).then_inc(windows_ready, 1)
            dve.wait_ge(windows_ready, 1)
            nwin = v.value_load(WPI[0:1, 0:1], min_val=1, max_val=NWIN)
            c = Chain(dve, count_c)

            def windows(w):
                c.step(v.tensor_copy(D0I, D0))
                c.step(v.tensor_tensor(TD, DSTF, D0[:, :].unsqueeze(2).to_broadcast([NP, NGROUP, ECH]), ALU.subtract))
                c.step(v.tensor_scalar(MK, TD, -0.5, None, ALU.is_gt))
                c.step(v.scalar_tensor_tensor(out=MK, in0=TD, scalar=WIN - 0.5, in1=MK, op0=ALU.is_lt, op1=ALU.mult))
                c.step(v.tensor_tensor(TD, TD, KEYA, ALU.add))
                v.tensor_scalar(D0, D0, float(WIN), None, ALU.add).then_inc(windows_ready, 1)
                dve.wait_ge(windows_ready, w + 2)
                dve.wait_ge(group_added, w * NGROUP + 2)
                dve.wait_ge(cnt_zero, 1)
                c.step(v.tensor_tensor(KEY, TD, MK, ALU.mult))
                dve.sem_inc(keys_known, 1)

            def onehots(w, g, s):
                v.tensor_tensor(OB[s][:, :, 0:NP], IOB[:, 0:NP].unsqueeze(1).to_broadcast([NP, ECH, NP]),
                                KEYBH[:, bass.ds(g, 1), :].rearrange("p o j -> p (o j)").unsqueeze(2).to_broadcast([NP, ECH, NP]), ALU.is_equal)
                for j in range(ECH):
                    dve.wait_ge(chunk_counted, (w * NGROUP + g) * ECH + (j + 1))
                    v.tensor_scalar(OK[j], IOK, KEY[:, bass.ds(g, 1), j:j + 1].rearrange("p a b -> p (a b)"), None,
                                    ALU.is_equal).then_inc(onehot_ready, 1)

            def window(g):
                return v.value_load(D0I[0:1, bass.ds(g, 1)], min_val=0, max_val=NODES - 1)

            def added(w, g, s, d0):
                dve.wait_ge(chunk_counted, (w * NGROUP + g) * ECH + (ECH + OHR))
                dve.wait_ge(group_added, w * NGROUP + g + 2)
                win = CNT3[:, :, bass.ds(d0, WIN)]
                v.tensor_tensor(win, ps[0:NP, 2 + s, 0:NT * WIN].rearrange("p (a b) -> p a b", b=WIN), win, ALU.add).then_inc(group_added, 1)

            def count_pair(t, more):
                g = t * PER_PAIR
                for j in range(PER_PAIR):
                    d0 = window(g + j)
                    if j + 1 < PER_PAIR or more:
                        onehots(0, g + (j + 1), (j + 1) % 2)
                    added(0, g + j, j % 2, d0)
                    if more and j == PER_PAIR - 3:
                        for s in range(2):
                            normalise(t * 2 + (s + 2), s)

            windows(0)
            onehots(0, 0, 0)
            with dve.Fori(0, NT // 2 - 1) as t:
                count_pair(t, True)
            count_pair(NT // 2 - 1, False)
            with dve.If(nwin > 1):
                with dve.Fori(1, nwin) as w:
                    c.enter(w - 1, 6)
                    windows(w)
                    onehots(w, 0, 0)
                    with dve.Fori(0, NGROUP // 2 - 1) as t:
                        first, second = window(t * 2), window(t * 2 + 1)
                        onehots(w, t * 2 + 1, 1)
                        added(w, t * 2, 0, first)
                        onehots(w, t * 2 + 2, 0)
                        added(w, t * 2 + 1, 1, second)
                    first, second = window(NGROUP - 2), window(NGROUP - 1)
                    onehots(w, NGROUP - 1, 1)
                    added(w, NGROUP - 2, 0, first)
                    added(w, NGROUP - 1, 1, second)
            dve.wait_ge(group_added, nwin * NGROUP + 2)
            c = Chain(dve, attend_c)
            v.memset(FLG[:, 0:1], 0.0).then_inc(cnt_done, 1)
            with dve.Fori(0, NT // 2) as t:
                for s in range(2):
                    dve.wait_ge(cntT_psum, t * 2 + s + 1 + 1)
                    v.tensor_scalar(NEGS[:, bass.ds(t * 2 + s, 1), :].rearrange("p o (a n) -> p (o a) n", n=NP), PST(0, NT, 4 * s)[0:NP], 0.5, NO_EDGE, ALU.is_lt, ALU.mult).then_inc(neg_ready, 1)
            dve.wait_ge(b1row_in, 16)
            dve.wait_ge(aw2_ready, 2 * KD)
            dve.wait_ge(neg_saved, 16 * NT)
            dve.wait_ge(als_stored, NT + 1)
            dve.wait_ge(h1_stored, NT + 1)

            def shift(al, j, done):
                c.step(v.tensor_scalar(TN[:, j:j + 1], M0[:, j:j + 1], 1 / SLOPE, al, ALU.mult, ALU.add))
                c.step(v.scalar_tensor_tensor(out=NM[:, j:j + 1], in0=TN[:, j:j + 1], scalar=SLOPE, in1=TN[:, j:j + 1],
                                              op0=ALU.mult, op1=ALU.max))
                v.scalar_tensor_tensor(out=NL[:, j:j + 1], in0=al, scalar=SLOPE, in1=NM[:, j:j + 1],
                                       op0=ALU.mult, op1=ALU.subtract).then_inc(done, 1)

            v.tensor_scalar(ALU8, ALD, 1 - SLOPE, None, ALU.mult).then_inc(ald_scaled, 1)

            def mask(i, h):
                if h == 0:
                    dve.wait_ge(neg_in, i * 16 + 16)
                dve.wait_ge(eT_psum, i * HEADS + (h + 1))
                dve.sem_inc(slot_taken, 1)
                v.tensor_tensor_reduce(out=TR[h % 4], in0=NEGC, in1=ALS[:, h, :], scale=SLOPE, scalar=MAX_FLOOR,
                                       op0=ALU.add, op1=ALU.max, accum_out=M0[:, h:h + 1]).then_inc(masked, 1)
                dve.wait_ge(masked, i * HEADS + (h + 1) + 1)
                shift(ALD[:, bass.ds(i, 1), h:h + 1].rearrange("p a b -> p (a b)"), h, shift_ready)

            def weights1(i, h):
                dve.wait_ge(eT_psum, i * HEADS + (h + 5))
                dve.wait_ge(o_psum, i * HEADS + (h + 1))
                v.tensor_tensor(PR[h % 2], PST(0, NT, 3 * (h % 2))[0:NP], CNT3[:, :, bass.ds(i * NP, NP)], ALU.mult).then_inc(p_ready, 1)

            def normalised(i):
                dve.wait_ge(o_psum, i * HEADS + (HEADS + 2))
                q = [ps[0:NP, 6 + f, 0:4 * (HC + 1)].rearrange("p (h c) -> p h c", c=HC + 1) for f in range(2)]
                for f in range(2):
                    c.step(v.tensor_scalar(RZ[:, 4 * f:4 * f + 4], q[f][:, :, HC:HC + 1].rearrange("p h c -> p (h c)"), EPS_Z, None, ALU.add))
                c.step(v.reciprocal(RZ, RZ))
                for f in range(2):
                    last = v.tensor_tensor(O1[:, f * HALF:f * HALF + HALF].rearrange("p (h c) -> p h c", c=HC), q[f][:, :, 0:HC],
                                           RZ[:, 4 * f:4 * f + 4].unsqueeze(2).to_broadcast([NP, 4, HC]), ALU.mult)
                    if f == 0:
                        c.step(last)
                last.then_inc(o_free, 1)

            def below(i):
                dve.wait_ge(o_free, i + 1)
                c.step(v.tensor_tensor(O1, O1, B1R, ALU.add))
                v.tensor_scalar(EL, O1, 0.0, None, ALU.min).then_inc(elu_in, 1)

            def elu(i):
                dve.wait_ge(elu_exp, i + 1)
                c.step(v.tensor_scalar(EL, EL, -1.0, None, ALU.add))
                v.scalar_tensor_tensor(out=O1, in0=O1, scalar=0.0, in1=EL, op0=ALU.max, op1=ALU.add).then_inc(o1_ready, 1)

            def tile1(i, before, more):
                for h in range(HEADS):
                    if h + 3 < HEADS:
                        mask(i, h + 3)
                    weights1(i, h)
                    if before and h < 3:
                        (normalised, below, elu)[h](i - 1)
                    if h + 4 >= HEADS and h + 1 < HEADS and more:
                        mask(i + 1, h + 4 - HEADS)

            for h in range(3):
                mask(0, h)
            tile1(0, False, True)
            with dve.Fori(1, NT - 1) as i:
                c.enter(i - 1, L1_STEPS)
                tile1(i, True, True)
            c.leave(NT - 2)
            tile1(NT - 1, True, False)
            normalised(NT - 1)
            below(NT - 1)
            elu(NT - 1)
            c = Chain(dve, second_c)
            dve.wait_ge(h2_stored, NT + 1)
            v.tensor_scalar(ALU8B, ALD2, 1 - SLOPE, None, ALU.mult).then_inc(ald2_scaled, 1)

            def mask2(i, s):
                dve.wait_ge(neg2_in, i * 16 + 16)
                dve.wait_ge(als2_stored, 1)
                dve.sem_inc(slot_taken, 1)
                v.tensor_tensor_reduce(out=TR[s], in0=NEGC, in1=ALS2, scale=SLOPE, scalar=MAX_FLOOR,
                                       op0=ALU.add, op1=ALU.max, accum_out=M0[:, s:s + 1]).then_inc(masked2, 1)
                dve.wait_ge(masked2, i + 1)
                shift(ALD2[:, bass.ds(i, 1)], s, shift2_ready)

            def weights2(i, s):
                dve.wait_ge(eT2_psum, i + 1)
                v.tensor_tensor(PR[s], PST(0, NT, 0)[0:NP], CNT3[:, :, bass.ds(i * NP, NP)], ALU.mult).then_inc(p2_ready, 1)

            def finish2(i, s):
                dve.wait_ge(o2_psum, i + 1)
                dve.wait_ge(xb_ready, i + 1)
                c.step(v.tensor_scalar(RZ[:, s:s + 1], ps[0:NP, 4 + 2 * s, HALF:HALF + 1], EPS_Z, None, ALU.add))
                c.step(v.reciprocal(RZ[:, s:s + 1], RZ[:, s:s + 1]))
                xi = X2[:, bass.ds(i, 1), :].rearrange("p o (f d) -> p (o f) d", f=2)
                c.step(v.scalar_tensor_tensor(out=xi, in0=ps[0:NP, 3 + 2 * s:5 + 2 * s, 0:HALF], scalar=RZ[:, s:s + 1], in1=xi,
                                              op0=ALU.mult, op1=ALU.add))
                for f in range(2):
                    dve.sem_inc(slot_taken, 1)
                    c.step(v.bn_stats(BS2[:, f, :], xi[:, f, :]))
                dve.sem_inc(slot_taken, 1)
                c.step(v.bn_aggr(MV1, BS2.rearrange("p f s -> p (f s)")))
                v.tensor_copy(MV[:, bass.ds(i, 1), :].rearrange("p o a -> p (o a)"), MV1).then_inc(x2_ready, 1)

            for s in range(2):
                mask2(s, s)
            weights2(0, 0)
            mask2(2, 0)
            with dve.Fori(0, (NT - 4) // 2) as t:
                c.enter(t, 2 * 6 + 2 * 2)
                for s in (1, 0):
                    i = t * 2 + (2 - s)
                    weights2(i, s)
                    finish2(i - 1, 1 - s)
                    mask2(i + 2, s)
            c.leave((NT - 4) // 2)
            for i in range(NT - 3, NT):
                weights2(i, i % 2)
                finish2(i - 1, (i - 1) % 2)
                if i + 2 < NT:
                    mask2(i + 2, i % 2)
            finish2(NT - 1, 1)
            c = Chain(dve, expert_c)
            dve.wait_ge(x2_ready, NT + 2)
            v.tensor_scalar(STD, MV[:, :, 1], EPS_LN, None, ALU.add).then_inc(var2_ready, 1)
            dve.wait_ge(std2_ready, 1)
            c.step(v.reciprocal(RSTD, STD))
            for s in range(ST):
                dve.wait_ge(sq_ready, s + 1)
                v.tensor_reduce(NRP[:, s, :, :], SQ[s % 2].rearrange("p k (n q) -> p k q n", q=PSLOT), AX_X, ALU.add).then_inc(sq_used, 1)
            dve.wait_ge(sq_used, ST)
            c.step(v.tensor_reduce(NRM.rearrange("p k q -> p (k q)"), NRP.rearrange("p s k q -> p (k q) s"), AX_X, ALU.add))
            dve.wait_ge(phT_stored, ST)
            v.tensor_scalar(NRM, NRM, EPS_PHI, None, ALU.add).then_inc(nrm_ready, 1)
            dve.wait_ge(nrs_ready, 1)
            c.step(v.reciprocal(NRR, NRM))
            for k in range(KD):
                kv = PHT[:, k, :].rearrange("p (n q) -> p n q", q=PSLOT)
                v.tensor_tensor(kv, kv, NRR[:, k:k + 1, :].to_broadcast([128, NEXP, PSLOT]), ALU.mult).then_inc(phn_ready, 1)
            dve.wait_ge(phn_ready, KD)
            dve.wait_ge(par_psum, 2)
            c = Chain(dve, logit_c)

            def centred(i, s):
                dve.wait_ge(xcT_psum, i + 1)
                dve.wait_ge(xh2_stored, i + 1)
                v.tensor_scalar(XC[s], X2[:, bass.ds(i, 1), :].rearrange("p o d -> p (o d)"),
                                MV[:, bass.ds(i, 1), 0:1].rearrange("p a b -> p (a b)"), RSTD[:, bass.ds(i, 1)],
                                ALU.subtract, ALU.mult).then_inc(xc_ready, 1)

            def slot_softmax(i, s):
                dve.wait_ge(lc_ready, i + 3)
                c.step(v.tensor_reduce(RM[s], LC[s], AX_X, ALU.max))
                v.tensor_scalar(RM[s], RM[s], -1.0, None, ALU.mult).then_inc(rm_ready, 1)
                dve.wait_ge(ce_ready, i + 1)
                c.step(v.reciprocal(RI[s], RS[s]))
                v.tensor_scalar(CC[s], CC[s], RI[s], None, ALU.mult).then_inc(cc_ready, 1)

            def node_max(i):
                dve.wait_ge(lT_psum, i + 3)
                v.tensor_reduce(CMX[:, :, bass.ds(i, 1)].rearrange("p a o -> p (a o)"), PSW(6, ST, NP), AX_X, ALU.max).then_inc(cm_taken, 1)

            for s in range(2):
                centred(s, s)
            centred(2, 0)
            slot_softmax(0, 0)
            AHEAD = 3
            with dve.Fori(0, (NT - 1 - AHEAD) // 2) as t:
                c.enter(t, 2 * 2)
                for s in (1, 0):
                    i = t * 2 + (2 - s)
                    node_max(i - 1)
                    centred(i + 2, s)
                    slot_softmax(i, s)
            c.leave((NT - 1 - AHEAD) // 2)
            for i in range(NT - AHEAD, NT):
                node_max(i - 1)
                if i + 2 < NT:
                    centred(i + 2, i % 2)
                slot_softmax(i, i % 2)
            node_max(NT - 1)
            dve.wait_ge(cm_taken, NT)
            c.step(v.tensor_reduce(CMN, CMX, AX_X, ALU.max))
            c.step(v.tensor_scalar(CMN, CMN, -1.0, None, ALU.mult))
            dve.wait_ge(lT_psum, NT + 2)
            dve.wait_ge(l_stored, NT + 2)
            v.tensor_tensor(DIAG, IDENT.unsqueeze(1).to_broadcast([128, ST, 128]), CMN.unsqueeze(2).to_broadcast([128, ST, 128]),
                            ALU.mult).then_inc(diag_ready, 1)
            dve.wait_ge(cmb_stored, 1)

            def less(s, p):
                dve.wait_ge(xs_psum, s + 1)
                v.tensor_tensor(DC[p], L[:, :, bass.ds(s * 128, 128)],
                                CMB[:, bass.ds(s * 128, 128)].unsqueeze(1).to_broadcast([NP, NT, 128]), ALU.add).then_inc(ds_ready, 1)

            def inputs(s, p):
                o = ps[:, 2 * p:2 * p + 2, 0:HALF]
                dve.wait_ge(xs_psum, s + 3)
                c.step(v.reciprocal(CSI, ps[:, 2 * p + 1, HALF:HALF + 1]))
                dve.wait_ge(xsT_psum, s + 1)
                c.step(v.tensor_scalar(XSW.rearrange("p (f d) -> p f d", f=2), o, CSI, None, ALU.mult))
                for f in range(2):
                    dve.sem_inc(slot_taken, 1)
                    c.step(v.bn_stats(SST[:, f, :], XSW[:, f * HALF:f * HALF + HALF]))
                dve.sem_inc(slot_taken, 1)
                c.step(v.bn_aggr(SMV, SST.rearrange("p f s -> p (f s)")))
                v.tensor_scalar(SSD, SMV[:, 1:2], EPS_LN, None, ALU.add).then_inc(xsv_ready, 1)
                dve.wait_ge(xstd_ready, s + 1)
                c.step(v.reciprocal(SRD, SSD))
                v.tensor_scalar(XSW, XSW, SMV[:, 0:1], SRD, ALU.subtract, ALU.mult).then_inc(xs_ready, 1)

            def gain(s, p):
                dve.wait_ge(xsT_psum, s + 2)
                xg = XGT[:, :, bass.ds(s * 128, 128)].rearrange("p k (n q) -> p k n q", q=PSLOT)
                c.step(v.tensor_tensor(xg, PSW(4 + 2 * p, KD).rearrange("p k (n q) -> p k n q", q=PSLOT),
                                       GT[:, :, bass.ds(s * GE, GE)].unsqueeze(3).to_broadcast([128, KD, GE, PSLOT]), ALU.mult))
                v.tensor_tensor(xg, xg, BT[:, :, bass.ds(s * GE, GE)].unsqueeze(3).to_broadcast([128, KD, GE, PSLOT]),
                                ALU.add).then_inc(xg_ready, 1)

            def body3(t, a, more):
                c.enter(t, 2 * 7)
                for s in range(2):
                    if more:
                        less(a + (s + 2), s)
                    inputs(a + s, s)
                    gain(a + s, s)

            dve.wait_ge(par_stored, 1)
            less(0, 0)
            less(1, 1)
            c = Chain(dve, input_c)
            with dve.Fori(0, ST // 2 - 1) as t:
                body3(t, t * 2, True)
            c.leave(ST // 2 - 1)
            body3(0, ST - 2, False)
            dve.wait_ge(xg_ready, ST + 1)
            dve.sem_inc(hb_ready, 1)
            dve.sem_inc(ys_ready, 1)
            dve.sem_inc(part_added, NPB)

            def hidden(g):
                dve.wait_ge(hT_psum, g + 2)
                dve.wait_ge(h_ready, g + 1)
                v.tensor_tensor(HB.rearrange("p k (e r) -> p k e r", r=PSLOT),
                                ps[:, 5:8, :].rearrange("p a (b e r) -> p (a b) e r", e=GE, r=PSLOT),
                                FB1T[:, :, bass.ds(g * GE, GE)].unsqueeze(3).to_broadcast([128, KH, GE, PSLOT]), ALU.add).then_inc(hb_ready, 1)

            def results(g):
                dve.wait_ge(w_used, w2_done(g))
                dve.wait_ge(b2g_in, g * (16 * GE) + 16 * GE)
                dve.wait_ge(part_psum, g * (2 * NT) + 1)
                v.tensor_tensor(YS.rearrange("p (f d) -> p f d", f=2), ps[:, 3:5, 0:HALF], B2G.rearrange("p (f d) -> p f d", f=2),
                                ALU.add).then_inc(ys_ready, 1)

            def onto(g):
                for n in range(2 * NT):
                    dve.wait_ge(part_psum, g * (2 * NT) + (n + 2))
                    xm = X2[:, n // 2, HALF * (n % 2):HALF * (n % 2) + HALF]
                    v.tensor_tensor(xm, ps[0:NP, 5 + n % NPB, 0:HALF], xm, ALU.add).then_inc(part_added, 1)

            with dve.Fori(0, 2) as t:
                hidden(t)
            with dve.Fori(0, ST - 2) as t:
                results(t)
                onto(t)
                hidden(t + 2)
            for g in range(ST - 2, ST):
                results(g)
                onto(g)


        @block.tensor
        def _(pe):
            m = nc.tensor
            for free in (xT_psum, cntT_psum):
                pe.sem_inc(free, 1)
            pe.wait_ge(ident_ready, 1)
            pe.wait_ge(wa_ready, 2 * KD)
            pe.sem_inc(chunk_counted, OHR)

            def flip(i, s):
                pe.wait_ge(xhat_ready, i + 1)
                for k in range(KD):
                    last = m.transpose(ps[:, k // 3, NP * (k % 3):NP * (k % 3) + NP], XH[s][:, 128 * k:128 * k + 128], IDENT[0:NP, 0:NP])
                last.then_inc(xT_psum, 1)

            def features(t, s, f):
                if f == 0:
                    pe.wait_ge(xT_ready, t * 2 + (s + 1))
                    pe.wait_ge(h1_stored, t * 2 + 1)
                    pe.wait_ge(als_stored, t * 2 + 1)
                for k in range(KD):
                    last = m.matmul(ps[0:NP, 4 + 2 * s + f, 0:HALF + 8], XT[s][:, k, :], W1A[:, k, f, :], start=(k == 0), stop=(k == KD - 1))
                if f == 1:
                    last.then_inc(h1_psum, 1)

            def spread_terms(t, s):
                pe.wait_ge(h1_stored, t * 2 + (s + 1) + 1)
                for h in range(HEADS):
                    last = m.matmul(ps[0:NP, 4 + 2 * s + h // 4, 128 * (h % 4):128 * (h % 4) + NP], ALSN[s][:, h:h + 1].to_broadcast([NP, NP]),
                                    IDENT[0:NP, 0:NP], start=True, stop=True)
                last.then_inc(als_psum, 1)

            def counted(w, g, s):
                pe.wait_ge(group_added, w * NGROUP + g + 1)
                for j in range(ECH):
                    pe.wait_ge(onehot_ready, (w * NGROUP + g) * ECH + (j + 1))
                    m.matmul(ps[0:NP, 2 + s, 0:NT * WIN], OB[s][:, j, 0:NP], OK[j], start=(j == 0), stop=(j == ECH - 1)).then_inc(chunk_counted, 1)

            with pe.Fori(0, NT // 2) as t:
                g = t * PER_PAIR
                flip(t * 2, 0)
                counted(0, g, 0)
                features(t, 0, 0)
                counted(0, g + 1, 1)
                features(t, 0, 1)
                flip(t * 2 + 1, 1)
                counted(0, g + 2, 0)
                spread_terms(t, 0)
                counted(0, g + 3, 1)
                features(t, 1, 0)
                counted(0, g + 4, 0)
                features(t, 1, 1)
                counted(0, g + 5, 1)
                spread_terms(t, 1)
                for j in range(6, PER_PAIR):
                    counted(0, g + j, j % 2)
            pe.wait_ge(als_stored, NT + 1)
            pe.wait_ge(windows_ready, 1)
            nwin = m.value_load(WPI[0:1, 0:1], min_val=1, max_val=NWIN)
            with pe.If(nwin > 1):
                with pe.Fori(1, nwin) as w:
                    with pe.Fori(0, NGROUP // 2) as t:
                        for s in range(2):
                            counted(w, t * 2 + s, s)
            with pe.Fori(0, NT // 2) as t:
                for s in range(2):
                    pe.wait_ge(cnt_tile, t * 2 + s + 1)
                    pe.wait_ge(neg_ready, t * 2 + 1)
                    for k in range(NT):
                        last = m.transpose(PST(k, 1, 4 * s)[0:NP, 0, :], CF[s][:, k, :], IDENT[0:NP, 0:NP])
                    last.then_inc(cntT_psum, 1)
            pe.wait_ge(neg_ready, NT + 1)
            pe.sem_inc(eT_psum, 4)
            pe.sem_inc(o_psum, 2)

            def turn(i, h):
                pe.wait_ge(e_ready, i * HEADS + (h + 1))
                if h >= 2 or not isinstance(i, int) or i > 0:
                    pe.wait_ge(p_ready, i * HEADS + (h - 1))
                for k in range(NT):
                    last = m.transpose(PST(k, 1, 3 * (h % 2))[0:NP, 0, :], TR[h % 4][:, NP * k:NP * k + NP], IDENT[0:NP, 0:NP])
                last.then_inc(eT_psum, 1)

            def gather(i, h):
                pe.wait_ge(p_ready, i * HEADS + (h + 1))
                for k in range(NT):
                    last = m.matmul(ps[0:NP, 6 + h // 4, (HC + 1) * (h % 4):(HC + 1) * (h % 4) + HC + 1], PR[h % 2][:, k, :], H1[:, k, h, :],
                                    start=(k == 0), stop=(k == NT - 1))
                last.then_inc(o_psum, 1)

            def flip1(i):
                pe.wait_ge(o1_ready, i + 1 + 1)
                for k in range(KD):
                    last = m.transpose(ps[:, k // 3, NP * (k % 3):NP * (k % 3) + NP], O1[:, 128 * k:128 * k + 128], IDENT[0:NP, 0:NP])
                last.then_inc(o1T_psum, 1)

            def project(i):
                pe.wait_ge(wa2_ready, 2 * KD)
                pe.wait_ge(o1T_ready, i + 1)
                for f in range(2):
                    for k in range(KD):
                        last = m.matmul(ps[0:NP, 3 + f, 0:HALF + 1], O1T[:, k, :], W2A[:, k, f, :], start=(k == 0), stop=(k == KD - 1))
                last.then_inc(h2_psum, 1)

            def tile1(i, before, more):
                for h in range(HEADS):
                    if before and h == 3:
                        flip1(i - 1)
                        gather(i, 3)
                        pe.wait_ge(o1T_ready, i)
                        turn(i, 4)
                        project(i - 1)
                    elif before and h == 4:
                        gather(i, 4)
                        pe.wait_ge(h2_stored, i + 1)
                        turn(i, 5)
                    else:
                        if h + 1 < HEADS:
                            turn(i, h + 1)
                        elif more:
                            turn(i + 1, 0)
                        if before and h == 0:
                            pe.wait_ge(o_free, i)
                        gather(i, h)

            turn(0, 0)
            tile1(0, False, True)
            with pe.Fori(1, NT - 1) as i:
                tile1(i, True, True)
            tile1(NT - 1, True, False)
            flip1(NT - 1)
            project(NT - 1)
            pe.wait_ge(h2_stored, NT + 1)
            for i in range(NT):
                last = m.matmul(PST(i, 1, 0)[0:NP, 0, :], ALS2N[:, i:i + 1].to_broadcast([NP, NP]), IDENT[0:NP, 0:NP], start=True, stop=True)
            last.then_inc(als2_psum, 1)
            pe.wait_ge(als2_stored, 1)
            pe.wait_ge(h2_ones, 1)

            def turn2(i, s):
                pe.wait_ge(e2_ready, i + 1)
                pe.wait_ge(p2_ready, i + 1)
                for k in range(NT):
                    last = m.transpose(PST(k, 1, 0)[0:NP, 0, :], TR[s][:, NP * k:NP * k + NP], IDENT[0:NP, 0:NP])
                last.then_inc(eT2_psum, 1)

            def gather2(i, s):
                pe.wait_ge(p2_ready, i + 2)
                pe.wait_ge(x2_ready, i + 1)
                for f in range(2):
                    for k in range(NT):
                        last = m.matmul(ps[0:NP, 3 + 2 * s + f, 0:HALF + f], PR[s][:, k, :], H2[:, k, f * HALF:f * HALF + HALF + f],
                                        start=(k == 0), stop=(k == NT - 1))
                last.then_inc(o2_psum, 1)

            def body(i, more):
                turn2(i + 1, 1)
                gather2(i, 0)
                if more:
                    turn2(i + 2, 0)
                gather2(i + 1, 1)

            pe.sem_inc(p2_ready, 1)
            pe.sem_inc(x2_ready, 2)
            turn2(0, 0)
            with pe.Fori(0, NT // 2 - 1) as t:
                body(t * 2, True)
            body(NT - 2, False)
            pe.wait_ge(x2_ready, NT + 2)
            pe.wait_ge(phi_in, 16)
            for s in range(ST):
                if s >= 2:
                    pe.wait_ge(phT_stored, s - 1)
                for k in range(KD):
                    last = m.transpose(PSW(2 * (s % 2), KD)[:, k, :], PHR[:, s, 128 * k:128 * k + 128], IDENT)
                last.then_inc(phT_psum, 1)
            pe.wait_ge(par_in, 48)
            for q in range(2):
                for k in range(KD):
                    last = m.transpose(ps[:, 4 + q, NEXP * k:NEXP * k + NEXP], LDP[q][:, 128 * k:128 * k + 128], IDENT[0:NEXP, 0:NEXP])
            last.then_inc(par_psum, 1)
            pe.wait_ge(phT_stored, ST)
            for k in range(KH):
                last = m.transpose(ps[:, k // 8, NEXP * (k % 8):NEXP * (k % 8) + NEXP], pairs(LDB, k), IDENT[0:NEXP, 0:NEXP])
            last.then_inc(par_psum, 1)
            pe.wait_ge(par_stored, 1)
            pe.wait_ge(phn_ready, KD)
            pe.sem_inc(xcT_psum, 2)
            pe.sem_inc(lT_psum, 2)
            pe.sem_inc(cT_psum, 2)

            def flip_x(i, s):
                pe.wait_ge(xc_ready, i + 1)
                pe.wait_ge(xcT_ready, i + 1)
                for k in range(KD):
                    last = m.transpose(ps[:, k // 3, NP * (k % 3):NP * (k % 3) + NP], XC[s][:, 128 * k:128 * k + 128], IDENT[0:NP, 0:NP])
                last.then_inc(xcT_psum, 1)

            def product(i, s):
                pe.wait_ge(xcT_ready, i + 2)
                pe.wait_ge(lc_ready, i + 1)
                for f in range(2):
                    for k in range(KD):
                        last = m.matmul(ps[0:NP, 2 + 2 * s + f, :], XCT[s][:, k, :], PHT[:, k, 512 * f:512 * f + 512], start=(k == 0), stop=(k == KD - 1))
                last.then_inc(l_psum, 1)

            def turn_l(i, s):
                pe.wait_ge(lc_ready, i + 3)
                pe.wait_ge(cT_stored, i + 1)
                for k in range(ST):
                    last = m.transpose(PSW(6, ST, NP)[:, k, :], LC[s][:, 128 * k:128 * k + 128], IDENT[0:NP, 0:NP])
                last.then_inc(lT_psum, 1)

            def turn_c(i, s):
                pe.wait_ge(cm_taken, i + 1)
                pe.wait_ge(cc_ready, i + 1)
                for k in range(ST):
                    last = m.transpose(PSW(6, ST, NP)[:, k, :], CC[s][:, 128 * k:128 * k + 128], IDENT[0:NP, 0:NP])
                last.then_inc(cT_psum, 1)

            for s in range(2):
                flip_x(s, s)
            product(0, 0)
            with pe.Fori(0, NT // 2 - 1) as t:
                for s in (1, 0):
                    i = t * 2 + (2 - s)
                    flip_x(i + 1, 1 - s)
                    turn_l(i - 1, 1 - s)
                    product(i, s)
                    turn_c(i - 1, 1 - s)
            turn_l(NT - 2, 0)
            product(NT - 1, 1)
            turn_c(NT - 2, 0)
            turn_l(NT - 1, 1)
            turn_c(NT - 1, 1)
            pe.wait_ge(diag_ready, 1)
            pe.wait_ge(ones_ready, 2)
            pe.wait_ge(cT_stored, NT + 1)
            for f in range(2):
                last = m.matmul(ps[0:NP, 4 + f, :], ONES[:, 0:NP], DIAG.rearrange("p a b -> p (a b)")[:, 512 * f:512 * f + 512], start=True, stop=True)
            last.then_inc(cmb_psum, 1)
            pe.wait_ge(cmb_stored, 1)
            pe.wait_ge(xh2_stored, NT + 2)
            pe.sem_inc(xs_psum, 2)
            pe.sem_inc(xsT_psum, 1)

            def sums(s, p):
                pe.wait_ge(dexp_ready, s + 1)
                pe.wait_ge(xs_ready, s + 1)
                for f in range(2):
                    for k in range(NT):
                        last = m.matmul(ps[:, 2 * p + f, 0:HALF + f], DC[p][:, k, :], XH2[:, k, f * HALF:f * HALF + HALF + f],
                                        start=(k == 0), stop=(k == NT - 1))
                last.then_inc(xs_psum, 1)

            def flip(s, p):
                pe.wait_ge(xs_ready, s + 3)
                pe.wait_ge(xg_ready, s + 1)
                for k in range(KD):
                    last = m.transpose(PSW(4 + 2 * p, KD)[:, k, :], XSW[:, 128 * k:128 * k + 128], IDENT)
                last.then_inc(xsT_psum, 1)

            def body(s, more):
                sums(s + 1, 1)
                flip(s, 0)
                if more:
                    sums(s + 2, 0)
                flip(s + 1, 1)

            pe.sem_inc(xs_ready, 2)
            pe.sem_inc(xg_ready, 1)
            sums(0, 0)
            with pe.Fori(0, ST // 2 - 1) as t:
                body(t * 2, True)
            body(ST - 2, False)
            pe.wait_ge(xg_ready, ST + 1)
            pe.wait_ge(xgs_zero, 2)
            for free in (hT_psum, part_psum):
                pe.sem_inc(free, 1)
            pe.sem_inc(w_used, RING)

            def up(g, phase):
                pe.wait_ge(xgs_ready, g * SUB + SUB)
                pe.wait_ge(hs_ready, g + 1)
                for u in range(USES):
                    k, b, slot = u // SUB, u % SUB, u % RING
                    pe.wait_ge(w_in[slot], phase * (32 * USES // RING) + 32 * (u // RING + 1))
                    for j in range(HID // 512):
                        for q in range(QUAD):
                            last = m.matmul(ps[32 * q:32 * q + 32, j, :], XGS[:, k, q, PSLOT * b:PSLOT * b + 32],
                                            RG[slot][:, q, 512 * j:512 * j + 512], start=(u == 0), stop=(u == USES - 1), skip_group_check=True)
                    last.then_inc(w_used, 1)

            def turn_h(g):
                pe.wait_ge(hs_ready, g + 2)
                pe.wait_ge(hb_ready, g + 1)
                for k in range(KH):
                    last = m.transpose(ps[:, 5 + k // 4, 128 * (k % 4):128 * (k % 4) + 128], pairs(HS, k), IDENT)
                last.then_inc(hT_psum, 1)

            def down(g, phase):
                pe.wait_ge(h_ready, g + 2)
                pe.wait_ge(ys_ready, g + 1)
                for u in range(USES):
                    k, b, slot = u // SUB, u % SUB, u % RING
                    pe.wait_ge(w_in[slot], phase * (32 * USES // RING) + 32 * (u // RING + 1))
                    for j in range(2):
                        for f in range(2):
                            for q in range(QUAD):
                                last = m.matmul(ps[32 * q:32 * q + 32, 3 + f, 0:HALF], HTS[:, 2 * k + j, q, PSLOT * b:PSLOT * b + 32],
                                                RG[slot][:, q, D * j + HALF * f:D * j + HALF * f + HALF],
                                                start=(u == 0 and j == 0), stop=(u == USES - 1 and j == 1), skip_group_check=True)
                    last.then_inc(w_used, 1)

            def combine(g):
                pe.wait_ge(ys_ready, g + 2)
                pe.wait_ge(ctc_ready, g + 1)
                for n in range(2 * NT):
                    i, f = n // 2, n % 2
                    pe.wait_ge(part_added, g * (2 * NT) + (n + 1))
                    m.matmul(ps[0:NP, 5 + n % NPB, 0:HALF], CTC[:, NP * i:NP * i + NP], YS[:, f * HALF:f * HALF + HALF],
                             start=True, stop=True).then_inc(part_psum, 1)

            with pe.Fori(0, 2) as t:
                up(t, t)
                turn_h(t)
            with pe.Fori(0, 1) as t:
                down(t, t + 2)
            with pe.Fori(0, ST - 2) as t:
                up(t + 2, t * 2 + 3)
                combine(t)
                pe.wait_ge(part_added, t * (2 * NT) + (2 * NT + NPB))
                turn_h(t + 2)
                down(t + 1, t * 2 + 4)
            with pe.Fori(ST - 2, ST - 1) as t:
                combine(t)
                down(t + 1, t * 2 + 3)
                combine(t + 1)



_INS = ["x", "src", "dst", "L0_gnn_W1", "L0_gnn_a_src1", "L0_gnn_a_dst1", "L0_gnn_b1", "L0_gnn_W2", "L0_gnn_a_src2",
        "L0_gnn_a_dst2", "L0_gnn_b2", "L0_ffn_phi", "L0_ffn_ln_g", "L0_ffn_ln_b", "L0_ffn_w1", "L0_ffn_b1",
        "L0_ffn_w2", "L0_ffn_b2"]
_OUTS = [((NODES, D), "float32")]


def kernel(**inputs):
    import numpy as _np
    import concourse.bacc as _bacc
    from concourse import mybir as _mybir
    from concourse.bass_utils import run_bass_kernel_spmd as _run

    nc = _bacc.Bacc("TRN2", target_bir_lowering=False, num_devices=1)
    arrays, args = {}, []
    for name in _INS:
        a = _np.ascontiguousarray(inputs[name])
        arrays[f"in_{name}_dram"] = a
        args.append(nc.dram_tensor(f"in_{name}_dram", a.shape, _mybir.dt.from_np(a.dtype), kind="ExternalInput").ap())
    for i, (shape, dtype) in enumerate(_OUTS):
        dt = _mybir.dt.from_np(_np.dtype(dtype))
        args.append(nc.dram_tensor(f"out_{i}_dram", shape, dt, kind="ExternalOutput").ap())
    gnn_ffn(nc, *args)
    r = _run(nc, [arrays], core_ids=[0])
    return r.results[0]["out_0_dram"]
```
